# Optimizing a Trainium2 kernel written in Bass

```python
import numpy as np
import jax
import jax.numpy as jnp

def _softmax(x, axis=-1):
    return jax.nn.softmax(x, axis=axis)

def _gelu(x):
    return jax.nn.gelu(x, approximate=True)

def _silu(x):
    return jax.nn.silu(x)

def _sigmoid(x):
    return jax.nn.sigmoid(x)

def _layernorm(x, axis=-1, eps=1e-05):
    m = jnp.mean(x, axis=axis, keepdims=True)
    v = jnp.var(x, axis=axis, keepdims=True)
    return (x - m) / jnp.sqrt(v + eps)

def _scatter_add(tgt, idx, src, axis=0):
    return tgt.at[idx].add(src)

def _segment_sum(src, seg, n):
    return jax.ops.segment_sum(src, seg, n)
kernel_name = 'mk_early_fusion_embed_d1_tok_img1024_r4_794f15'

def setup_inputs(seed: int=0):
    np.random.seed(seed)
    _w = jnp.asarray

    def _rec_inputs():
        import jax
        import jax.numpy as jnp
        _rk = jax.random.key(seed)
        x = 7.57192e-06 + 1.00007 * jax.random.normal(jax.random.fold_in(_rk, 1), (16, 3, 96, 96), jnp.float32)
        x_txt = jax.random.randint(jax.random.fold_in(_rk, 51), (16, 32), 0, 127998, jnp.int32)
        return (x, x_txt)
    x, x_txt = _rec_inputs()

    def _L0_tok_setup():
        import jax, jax.numpy as jnp
        import numpy as np
        IMG = 224
        PATCH = 16
        C_IN = 3
        D = 256
        B = 64
        PATCH_DIM = C_IN * PATCH * PATCH
        key = jax.random.key(seed)
        k1, k2, k3 = jax.random.split(key, 3)
        x = jax.random.normal(k1, (B, C_IN, IMG, IMG), dtype=jnp.float32)
        W = jax.random.normal(k2, (D, PATCH_DIM), dtype=jnp.float32) * (1.0 / np.sqrt(PATCH_DIM))
        b = jax.random.normal(k3, (D,), dtype=jnp.float32) * 0.02
        return {'x': x, 'W': W, 'b': b}
    _L0_tok_all = _L0_tok_setup()
    _L0_tok_in = {k: v for k, v in _L0_tok_all.items() if k in ('W', 'b')}
    del _L0_tok_all

    def _L0_txt_setup():
        import jax, jax.numpy as jnp
        import numpy as np
        VOCAB, K, DIM = (32000, 128, 256)
        PADDING_IDX = 1
        key = jax.random.key(seed)
        k1, k2, k3 = jax.random.split(key, 3)
        inp = jax.random.randint(k1, (4, 1024), 0, VOCAB, dtype=jnp.int64)
        weight_l = jax.random.normal(k2, (VOCAB, K), dtype=jnp.float32) * 0.02
        weight_r = jax.random.normal(k3, (K, DIM), dtype=jnp.float32) * 0.02
        return {'input': inp, 'weight_l': weight_l, 'weight_r': weight_r}
    _L0_txt_all = _L0_txt_setup()
    _L0_txt_in = {k: v for k, v in _L0_txt_all.items() if k in ('weight_l', 'weight_r')}
    del _L0_txt_all

    def _L0_attn_setup():
        import jax, jax.numpy as jnp
        import numpy as np
        D_MODEL, D_K, D_V, N_HEADS = (256, 64, 64, 16)
        B, T = (4, 512)

        def _xavier(key, shape, gain):
            fan_in, fan_out = (shape[0], shape[1])
            a = gain * np.sqrt(6.0 / (fan_in + fan_out))
            return jax.random.uniform(key, shape, jnp.float32, -a, a)
        key = jax.random.key(seed)
        ks = jax.random.split(key, 6)
        H, dk, dv, d = (N_HEADS, D_K, D_V, D_MODEL)
        return {'x': jax.random.normal(ks[0], (B, T, d), jnp.float32), 'W_q': _xavier(ks[1], (d, H * dk), 0.1), 'W_k': _xavier(ks[2], (d, H * dk), 0.1), 'W_v': _xavier(ks[3], (d, H * dv), 0.1), 'W_gate': _xavier(ks[4], (d, H * dk), 0.01), 'b_gate': jnp.full((H * dk,), 3.0, jnp.float32), 'W_o': _xavier(ks[5], (H * dv, d), 0.1)}
    _L0_attn_all = _L0_attn_setup()
    _L0_attn_in = {k: v for k, v in _L0_attn_all.items() if k in ('W_q', 'W_k', 'W_v', 'W_gate', 'b_gate', 'W_o')}
    del _L0_attn_all

    def _L0_ffn_setup():
        import jax, jax.numpy as jnp
        import numpy as np
        E = 8
        D = 256
        H = 512
        TOP_K = 2
        key = jax.random.key(seed)
        k_x, k_g, k_w1, k_w2 = jax.random.split(key, 4)
        B, S = (4, 512)
        inp = {'input': jax.random.normal(k_x, (B, S, D), dtype=jnp.float32), 'Wg': jax.random.normal(k_g, (D, E), dtype=jnp.float32) * 0.02, 'W1': jax.random.normal(k_w1, (E, D, H), dtype=jnp.float32) * 0.02, 'b1': jnp.zeros((E, H), dtype=jnp.float32), 'W2': jax.random.normal(k_w2, (E, H, D), dtype=jnp.float32) * 0.02, 'b2': jnp.zeros((E, D), dtype=jnp.float32)}
        return inp
    _L0_ffn_all = _L0_ffn_setup()
    _L0_ffn_in = {k: v for k, v in _L0_ffn_all.items() if k in ('Wg', 'W1', 'b1', 'W2', 'b2')}
    del _L0_ffn_all
    return {'x': x, 'x_txt': x_txt, 'L0_tok_W': _L0_tok_in['W'], 'L0_tok_b': _L0_tok_in['b'], 'L0_txt_weight_l': _L0_txt_in['weight_l'], 'L0_txt_weight_r': _L0_txt_in['weight_r'], 'L0_attn_W_q': _L0_attn_in['W_q'], 'L0_attn_W_k': _L0_attn_in['W_k'], 'L0_attn_W_v': _L0_attn_in['W_v'], 'L0_attn_W_gate': _L0_attn_in['W_gate'], 'L0_attn_b_gate': _L0_attn_in['b_gate'], 'L0_attn_W_o': _L0_attn_in['W_o'], 'L0_ffn_Wg': _L0_ffn_in['Wg'], 'L0_ffn_W1': _L0_ffn_in['W1'], 'L0_ffn_b1': _L0_ffn_in['b1'], 'L0_ffn_W2': _L0_ffn_in['W2'], 'L0_ffn_b2': _L0_ffn_in['b2']}

def reference(x, x_txt, L0_tok_W, L0_tok_b, L0_txt_weight_l, L0_txt_weight_r, L0_attn_W_q, L0_attn_W_k, L0_attn_W_v, L0_attn_W_gate, L0_attn_b_gate, L0_attn_W_o, L0_ffn_Wg, L0_ffn_W1, L0_ffn_b1, L0_ffn_W2, L0_ffn_b2):
    import jax
    import jax.numpy as jnp

    def _L0_tok_ref(x, W, b):
        import jax, jax.numpy as jnp
        import numpy as np
        IMG = 224
        PATCH = 16
        C_IN = 3
        D = 256
        B = 64
        PATCH_DIM = C_IN * PATCH * PATCH
        Bx, C, H, Wd = x.shape
        p = PATCH
        Hp, Wp = (H // p, Wd // p)
        patches = x.reshape(Bx, C, Hp, p, Wp, p).transpose(0, 2, 3, 1, 4, 5)
        patches = patches.reshape(Bx, -1, PATCH_DIM)
        return jnp.einsum('bnp,dp->bnd', patches, W) + b

    def _L0_txt_ref(input, weight_l, weight_r):
        import jax, jax.numpy as jnp
        import numpy as np
        VOCAB, K, DIM = (32000, 128, 256)
        PADDING_IDX = 1
        weight = weight_l @ weight_r
        return weight[input]

    def _L0_attn_ref(x, W_q, W_k, W_v, W_gate, b_gate, W_o):
        import jax, jax.numpy as jnp
        import numpy as np
        D_MODEL, D_K, D_V, N_HEADS = (256, 64, 64, 16)
        B, T = (4, 512)

        def _xavier(key, shape, gain):
            fan_in, fan_out = (shape[0], shape[1])
            a = gain * np.sqrt(6.0 / (fan_in + fan_out))
            return jax.random.uniform(key, shape, jnp.float32, -a, a)
        Bn, Tn, d = x.shape
        H, dk, dv = (N_HEADS, D_K, D_V)
        q = (x @ W_q).reshape(Bn, Tn, H, dk)
        k = (x @ W_k).reshape(Bn, Tn, H, dk)
        v = (x @ W_v).reshape(Bn, Tn, H, dv)
        a = jax.nn.sigmoid(x @ W_gate + b_gate).reshape(Bn, Tn, H, dk)

        def step(S, qkva):
            q_t, k_t, v_t, a_t = qkva
            S = a_t[..., None] * S + k_t[..., None] * v_t[..., None, :]
            o_t = jnp.einsum('bhk,bhkv->bhv', q_t, S)
            return (S, o_t)
        S0 = jnp.zeros((Bn, H, dk, dv), x.dtype)
        qs = jnp.moveaxis(q, 1, 0)
        ks_ = jnp.moveaxis(k, 1, 0)
        vs = jnp.moveaxis(v, 1, 0)
        as_ = jnp.moveaxis(a, 1, 0)
        _, outs = jax.lax.scan(step, S0, (qs, ks_, vs, as_))
        out = jnp.moveaxis(outs, 0, 1).reshape(Bn, Tn, H * dv)
        return out @ W_o

    def _L0_ffn_ref(input, Wg, W1, b1, W2, b2):
        import jax, jax.numpy as jnp
        import numpy as np
        E = 8
        D = 256
        H = 512
        TOP_K = 2
        logits = jnp.einsum('bsd,de->bse', input, Wg)
        probs = jax.nn.softmax(logits, axis=-1)
        top_vals, top_idx = jax.lax.top_k(probs, TOP_K)
        top_vals = top_vals / jnp.sum(top_vals, axis=-1, keepdims=True)
        onehot = jax.nn.one_hot(top_idx, E, dtype=input.dtype)
        mask = jnp.sum(onehot, axis=2)
        scores = jnp.sum(onehot * top_vals[..., None], axis=2)
        xm = input[None] * jnp.moveaxis(mask, -1, 0)[..., None]
        h = jnp.einsum('ebsd,edh->ebsh', xm, W1) + b1[:, None, None, :]
        h = jax.nn.relu(h)
        y = jnp.einsum('ebsh,ehd->ebsd', h, W2) + b2[:, None, None, :]
        out = jnp.sum(y * jnp.moveaxis(scores, -1, 0)[..., None], axis=0)
        return out
    h = _L0_tok_ref(x, L0_tok_W, L0_tok_b)
    h = jnp.concatenate([h, _L0_txt_ref(x_txt, L0_txt_weight_l, L0_txt_weight_r)], axis=1)
    h = h + _L0_attn_ref(_layernorm(h, axis=-1), L0_attn_W_q, L0_attn_W_k, L0_attn_W_v, L0_attn_W_gate, L0_attn_b_gate, L0_attn_W_o)
    h = h + _L0_ffn_ref(_layernorm(h, axis=-1), L0_ffn_Wg, L0_ffn_W1, L0_ffn_b1, L0_ffn_W2, L0_ffn_b2)
    return h

_drawn_inputs = setup_inputs


def setup_inputs(seed=0):
    import zlib

    import numpy as np

    out = dict(_drawn_inputs(seed))
    spreads = {'L0_attn_b_gate': (3.0, 0.2), 'L0_ffn_b1': (0.0, 0.27), 'L0_ffn_b2': (0.0, 0.1)}
    factors = {'L0_attn_W_gate': 200.0}
    for name, (base, spread) in spreads.items():
        noise = np.random.default_rng([zlib.crc32(name.encode()), seed]).standard_normal(out[name].shape)
        drawn = base * np.exp(spread * noise) if base else spread * noise
        out[name] = jnp.asarray(drawn.astype(out[name].dtype))
    for name, factor in factors.items():
        out[name] = (out[name] * factor).astype(out[name].dtype)
    return out
```

```python
from contextlib import ExitStack

import numpy as np

import concourse.bass as bass
from concourse import mybir

F32 = mybir.dt.float32
F32R = mybir.dt.float32r
I32 = mybir.dt.int32
U32 = mybir.dt.uint32
ALU = mybir.AluOpType
ACT = mybir.ActivationFunctionType
AX_X = mybir.AxisListType.X

P = 128
B, NP, NT = 16, 36, 32
T = NP + NT
TOK = B * T
D, PD = 256, 768
KE = 128
VOCAB = 32000
H, DK = 16, 64
HP = H // 2
E, FH = 8, 512
DC, PC, FC = D // P, PD // P, FH // P
HALF = TOK // 2
GB = 4
G = B // GB
GT = GB * T
HB = B // 2
U_LIMIT = 1e25
LN_EPS = 1e-5
MATS = 4
GATE, KEY, QUERY, VALUE = range(MATS)
WA = MATS * DC * P
WF = DC * FH
FPACK = 2 * WF + FC + DC
RT = -(-TOK // P)


def build(nc, x_idx, patches, w_tok, b_tok, w_l, w_r, w_attn, w_o, w_gate, w_ffn, out, scores_dram):
    with ExitStack() as ctx:
        def sem(name):
            return ctx.enter_context(nc.semaphore(name))

        cursor = [16512]

        def sb(name, shape, dt=F32, at=None):
            c = cursor if at is None else at
            t = nc.alloc_sbuf_tensor_at(name, shape, dt, offset=c[0])
            c[0] += -(-int(np.prod(shape[1:])) * 4 // 32) * 32
            assert c[0] <= nc.sbuf_usable_end
            return t

        hT = sb("hT", [P, DC, TOK])
        xnhi = sb("xnhi", [P, DC, TOK], F32R)
        xnlo = sb("xnlo", [P, DC, TOK], F32R)
        oT = sb("oT", [P, HP, TOK])
        wo = sb("wo", [P, HP, D])
        causal = sb("causal", [P, 2, GT])
        causal_bits = sb("causal_bits", [P, 2, GT], U32)
        first = sb("first", [P, HALF])
        ident = sb("ident", [P, P])
        mean_w = sb("mean_w", [P, P])
        ones = sb("ones", [P, 1])
        eps = sb("eps", [P, 1])
        btok = sb("btok", [P, DC])
        u_ok = sb("u_ok", [P, B])
        ok_col = sb("ok_col", [P, 1])
        ok_sum = sb("ok_sum", [1, 1], I32)
        wg = sb("wg", [P, DC, E])
        wghi = sb("wghi", [P, DC, E], F32R)
        wglo = sb("wglo", [P, DC, E], F32R)
        iota_e = sb("iota_e", [P, RT, E])
        lg = sb("lg", [P, RT, E])
        pr = sb("pr", [P, RT, E])
        top = sb("top", [P, RT, 8])
        topi = sb("topi", [P, RT, 8], U32)
        topf = sb("topf", [P, RT, 8])
        pick = sb("pick", [P, 2, RT, E])
        rs = sb("rs", [P, 4, RT])
        sc = sb("sc", [P, RT, E])
        scT = sb("scT", [E, TOK])
        idx_i = sb("idx_i", [P, G], I32)
        idx_f = sb("idx_f", [P, G])
        idx_n = sb("idx_n", [P, G])
        idx_u = sb("idx_u", [P, G], U32)

        start = cursor[0]
        pt = sb("pt", [P, 2, PC, HB * NP])
        wtok = sb("wtok", [P, PC, D])
        gath = sb("gath", [P, G, KE])
        gT = sb("gT", [P, B * NT])
        wr = sb("wr", [P, D])
        over = [start]
        fraw = [sb(f"fraw{i}", [P, FPACK], at=over) for i in range(2)]
        assert over[0] <= cursor[0]

        start = cursor[0]
        e_g = sb("e_g", [P, TOK])
        u_g = sb("u_g", [P, TOK])
        U = sb("U", [P, TOK])
        A = sb("A", [P, TOK])
        qraw = sb("qraw", [P, TOK])
        kU = [sb(f"kU{i}", [P, TOK]) for i in range(2)]
        ln_end = cursor[0]
        qA = [sb(f"qA{i}", [P, TOK]) for i in range(2)]
        vb = [sb(f"vb{i}", [P, B, P]) for i in range(2)]
        pb = [sb(f"pb{i}", [P, 2, GT]) for i in range(2)]
        pb_end = cursor[0]
        wraw = [sb(f"wraw{i}", [P, WA + 1]) for i in range(2)]
        bneg = [sb(f"bneg{i}", [P, 1]) for i in range(2)]
        whi = [sb(f"whi{i}", [P, MATS, DC, P], F32R) for i in range(2)]
        wlo = [sb(f"wlo{i}", [P, MATS, DC, P], F32R) for i in range(2)]
        attn_end = cursor[0]
        over = [start]
        xc = sb("xc", [P, 2, DC, HALF], at=over)
        sq = sb("sq", [P, 2, DC, HALF], at=over)
        std = sb("std", [P, 2, HALF], at=over)
        rstd = sb("rstd", [P, 2, HALF], at=over)
        over = [start]
        h1hi = sb("h1hi", [P, 2, FC, HALF], F32R, at=over)
        h1lo = sb("h1lo", [P, 2, FC, HALF], F32R, at=over)
        f1hi = [sb(f"f1hi{i}", [P, DC, FH], F32R, at=over) for i in range(2)]
        f1lo = [sb(f"f1lo{i}", [P, DC, FH], F32R, at=over) for i in range(2)]
        f2hi = [sb(f"f2hi{i}", [P, FC, D], F32R, at=over) for i in range(2)]
        f2lo = [sb(f"f2lo{i}", [P, FC, D], F32R, at=over) for i in range(2)]
        fbias = [sb(f"fbias{i}", [P, FC + DC], at=over) for i in range(2)]
        hf = [sb(f"hf{i}", [P, HALF], at=over) for i in range(2)]
        ytmp = [sb(f"ytmp{i}", [P, HALF], at=over) for i in range(2)]
        scb = [sb(f"scb{i}", [P, TOK], at=over) for i in range(2)]
        cursor[0] = max(cursor[0], over[0])
        over = [start]
        gx = sb("gx", [P, DC, TOK], at=over)
        gq, ga, gsum, gprod = (sb(n, [P, TOK], at=over) for n in ("gq", "ga", "gsum", "gprod"))
        gk = [sb(f"gk{i}", [P, TOK], at=over) for i in range(2)]
        gv = [sb(f"gv{i}", [P, TOK], at=over) for i in range(2)]
        head_sum = sb("head_sum", [P, P], at=over)
        assert over[0] <= pb_end
        assert cursor[0] <= nc.sbuf_usable_end, cursor[0]

        ps = ctx.enter_context(nc.psum_tensor("ps", [P, 8, 512], F32))

        def slot(k, n=GT):
            return ps[:, 2 * k:2 * k + 2, 0:n]

        def half(t, c, lead=()):
            return t[(slice(None),) + lead + (slice(c * HALF, (c + 1) * HALF),)].rearrange(
                "p (j n) -> p j n", j=2)

        def banks(t):
            return t.rearrange("p (j n) -> p j n", j=2)

        s_idx_in, s_idx, s_gath = sem("s_idx_in"), sem("s_idx"), sem("s_gath")
        s_pt = [sem("s_pt0"), sem("s_pt1")]
        s_wtok, s_wr, s_wo, s_wg = sem("s_wtok"), sem("s_wr"), sem("s_wo"), sem("s_wg")
        s_const = sem("s_const")
        s_gt_mm, s_gt, s_emb_mm, s_emb = sem("s_gt_mm"), sem("s_gt"), sem("s_emb_mm"), sem("s_emb")
        s_txt = sem("s_txt")
        s_mean, s_xc, s_sq, s_var, s_std = sem("s_mean"), sem("s_xc"), sem("s_sq"), sem("s_var"), sem("s_std")
        s_rstd, s_xn, s_xnhi, s_xnlo = sem("s_rstd"), sem("s_xn"), sem("s_xnhi"), sem("s_xnlo")
        s_wload = [sem("s_wload0"), sem("s_wload1")]
        s_whi, s_wlo = sem("s_whi"), sem("s_wlo")
        s_proj, s_exp, s_u, s_scan, s_ku = sem("s_proj"), sem("s_exp"), sem("s_u"), sem("s_scan"), sem("s_ku")
        s_uok, s_qraw, s_a, s_qa = sem("s_uok"), sem("s_qraw"), sem("s_a"), sem("s_qa")
        s_vmm, s_v, s_pmm, s_p, s_omm, s_o = (sem(n) for n in ("s_vmm", "s_v", "s_pmm", "s_p", "s_omm", "s_o"))
        s_okcol, s_okmm, s_ok, s_way = sem("s_okcol"), sem("s_okmm"), sem("s_ok"), sem("s_way")
        s_womm, s_h2 = sem("s_womm"), sem("s_h2")
        s_wgs, s_lgmm, s_prob, s_exps, s_sc, s_sctmm, s_sct = (
            sem(n) for n in ("s_wgs", "s_lgmm", "s_prob", "s_exps", "s_sc", "s_sctmm", "s_sct"))
        s_scd = sem("s_scd")
        s_scb = [sem("s_scb0"), sem("s_scb1")]
        s_fload = [sem("s_fload0"), sem("s_fload1")]
        s_f1hi, s_f1lo, s_f2hi, s_f2lo = sem("s_f1hi"), sem("s_f1lo"), sem("s_f2hi"), sem("s_f2lo")
        s_w1mm, s_relu, s_h1hi, s_h1lo = sem("s_w1mm"), sem("s_relu"), sem("s_h1hi"), sem("s_h1lo")
        s_w2mm, s_comb, s_acc = sem("s_w2mm"), sem("s_comb"), sem("s_acc")
        s_out = sem("s_out")
        s_gw, s_gset, s_gproj, s_gread, s_gterm, s_gbc, s_gdone = (
            sem(n) for n in ("s_gw", "s_gset", "s_gproj", "s_gread", "s_gterm", "s_gbc", "s_gdone"))
        s_link, s_link2, s_first = sem("s_link"), sem("s_link2"), sem("s_first")

        block = ctx.enter_context(nc.Block())

        def early(n, count):
            return isinstance(n, int) and n < count

        @block.sync
        def _(sp):
            sp.dma_start(idx_i[:], x_idx).then_inc(s_idx_in, 16)
            sp.dma_start(wtok[:], w_tok).then_inc(s_wtok, 16)
            for c in range(2):
                sp.dma_start(pt[:, c], patches[c]).then_inc(s_pt[c], 16)
            sp.dma_start(wr[:], w_r).then_inc(s_wr, 16)
            sp.dma_start(btok[:], b_tok).then_inc(s_wr, 16)
            for hp in range(HP):
                if hp >= 2:
                    sp.wait_ge(s_wlo, hp - 1)
                sp.dma_start(wraw[hp % 2][:], w_attn[hp]).then_inc(s_wload[hp % 2], 16)
                if hp == 1:
                    sp.dma_start(wo[:], w_o).then_inc(s_wo, 16)
                    sp.dma_start(wg[:], w_gate).then_inc(s_wg, 16)
            for e in range(2):
                sp.dma_start(fraw[e][:], w_ffn[e]).then_inc(s_fload[e], 16)
            sp.wait_ge(s_ok, 1)
            in_range = sp.value_load(ok_sum[0:1, 0:1], min_val=0, max_val=P)
            with sp.If(in_range < P):
                with sp.Fori(0, HP) as hp:
                    sp.wait_ge(s_gdone, hp + 1)
                    sp.dma_start(wraw[0][:], w_attn[bass.ds(hp, 1)].rearrange("o p n -> (o p) n")
                                 ).then_inc(s_gw, 16)
            sp.wait_ge(s_sct, 1)
            sp.dma_start(scores_dram, scT[:]).then_inc(s_scd, 16)
            sp.wait_ge(s_scd, 16)
            for e in range(E):
                if e >= 2:
                    sp.wait_ge(s_comb, 4 * (e - 1))
                sp.dma_start(scb[e % 2][:], scores_dram[e:e + 1, :].to_broadcast([P, TOK])
                             ).then_inc(s_scb[e % 2], 16)
                if e + 2 < E:
                    sp.wait_ge(s_f2lo, e + 1)
                    sp.dma_start(fraw[e % 2][:], w_ffn[e + 2]).then_inc(s_fload[e % 2], 16)
            for c in range(2):
                sp.wait_ge(s_acc, 4 * (E - 1) + 2 * (c + 1))
                sp.dma_start(out[:, :, c * HALF:(c + 1) * HALF],
                             hT[:, :, c * HALF:(c + 1) * HALF]).then_inc(s_out, 16)
            sp.wait_ge(s_out, 32)

        def three(pe, outs, pairs):
            for n, dst in enumerate(outs):
                for i, (shi, slo, mhi, mlo) in enumerate(pairs):
                    pe.matmul(dst, slo, mhi[n], start=(i == 0), stop=False)
                    pe.matmul(dst, shi, mlo[n], start=False, stop=False)
                    last = pe.matmul(dst, shi, mhi[n], start=False, stop=(i == len(pairs) - 1))
            return last

        @block.tensor
        def _(pe):
            pe.wait_ge(s_wtok, 16)
            for c in range(2):
                pe.wait_ge(s_pt[c], 16)
                for m in range(DC):
                    for k in range(PC):
                        last = pe.matmul(ps[:, 4 * c + m, 0:HB * NP], wtok[:, k, m * P:(m + 1) * P],
                                         pt[:, c, k, :], start=(k == 0), stop=(k == PC - 1))
                    last.then_inc(s_emb_mm, 1)
            pe.wait_ge(s_const, 5)
            for g in range(G):
                pe.wait_ge(s_gath, 16 * (g + 1))
                last = pe.transpose(ps[:, 7, g * P:(g + 1) * P], gath[:, g, :], ident[:])
            last.then_inc(s_gt_mm, 1)
            pe.wait_ge(s_gt, 1)
            pe.wait_ge(s_wr, 32)
            for c in range(2):
                for m in range(DC):
                    pe.matmul(ps[:, 4 * c + 2 + m, 0:HB * NT], wr[:, m * P:(m + 1) * P],
                              gT[:, c * HB * NT:(c + 1) * HB * NT], start=True, stop=True
                              ).then_inc(s_emb_mm, 1)

            def stats(k):
                for c in range(2):
                    n = 2 * k + c
                    if k == 0:
                        pe.wait_ge(s_emb, 2 * (c + 1))
                        pe.wait_ge(s_txt, 2 * (c + 1))
                    else:
                        pe.wait_ge(s_h2, 2 * (c + 1))
                    for j in range(2):
                        for m in range(DC):
                            last = pe.matmul(ps[:, 4 * c + j, 0:GT], mean_w[:], half(hT, c, (m,))[:, j, :],
                                             start=(m == 0), stop=(m == DC - 1))
                    last.then_inc(s_mean, 1)
                    if c == 1:
                        variance(k, 0)
                variance(k, 1)

            def variance(k, c):
                pe.wait_ge(s_sq, 2 * k + c + 1)
                for j in range(2):
                    for m in range(DC):
                        last = pe.matmul(ps[:, 4 * c + 2 + j, 0:GT], mean_w[:], banks(sq[:, c, m, :])[:, j, :],
                                         start=(m == 0), stop=(m == DC - 1))
                last.then_inc(s_var, 1)

            def project(hp, par, mat, c):
                pairs = [(whi[par][:, mat, m, :], wlo[par][:, mat, m, :],
                          [half(xnhi, c, (m,))[:, j, :] for j in range(2)],
                          [half(xnlo, c, (m,))[:, j, :] for j in range(2)]) for m in range(DC)]
                three(pe, [ps[:, 2 * c + j, 0:GT] for j in range(2)], pairs).then_inc(s_proj, 1)

            def projections(hp, par):
                pe.wait_ge(s_wlo, hp + 1)
                for c in range(2):
                    if not early(hp, 1):
                        pe.wait_ge(s_qraw, 2 * hp - 1 + c)
                    project(hp, par, GATE, c)
                for c in range(2):
                    pe.wait_ge(s_exp, 2 * hp + 1 + c)
                    project(hp, par, KEY, c)
                for c in range(2):
                    pe.wait_ge(s_ku, 2 * hp + 1 + c)
                    project(hp, par, QUERY, c)

            def values(hp, par, g):
                if not (early(hp, 1) and g == 0):
                    pe.wait_ge(s_v, 4 * hp + g)
                for b in range(GB):
                    t = slice((GB * g + b) * T, (GB * g + b + 1) * T)
                    dst = ps[0:T, 6, b * P:(b + 1) * P]
                    for m in range(DC):
                        pe.matmul(dst, xnlo[:, m, t], whi[par][:, VALUE, m, :], start=(m == 0), stop=False)
                        pe.matmul(dst, xnhi[:, m, t], wlo[par][:, VALUE, m, :], start=False, stop=False)
                        last = pe.matmul(dst, xnhi[:, m, t], whi[par][:, VALUE, m, :],
                                         start=False, stop=(m == DC - 1))
                last.then_inc(s_vmm, 1)

            def pair_scores(a, par, g):
                pe.wait_ge(s_qa, 2 * a + 1 + g // 2)
                if not (early(a, 1) and g == 0):
                    pe.wait_ge(s_p, 4 * a + g)
                for h in range(2):
                    rows = slice(DK * h, DK * (h + 1))
                    for b in range(GB):
                        t = slice((GB * g + b) * T, (GB * g + b + 1) * T)
                        last = pe.matmul(ps[0:T, 4 + h, b * T:(b + 1) * T], kU[par][rows, t], qA[par][rows, t],
                                         start=True, stop=True)
                last.then_inc(s_pmm, 1)

            def mix(a, par, g):
                pe.wait_ge(s_p, 4 * a + g + 1)
                pe.wait_ge(s_v, 4 * a + g + 1)
                if not (early(a, 1) and g == 0):
                    pe.wait_ge(s_o, 4 * a + g)
                for b in range(GB):
                    for h in range(2):
                        last = pe.matmul(ps[DK * h:DK * (h + 1), 7, b * T:(b + 1) * T],
                                         vb[par][0:T, GB * g + b, DK * h:DK * (h + 1)],
                                         pb[g % 2][0:T, h, b * T:(b + 1) * T], start=True, stop=True)
                last.then_inc(s_omm, 1)

            def pair_step(hp, par):
                projections(hp, par)
                pair_scores(hp - 1, 1 - par, 0)
                for g in range(G):
                    values(hp, par, g)
                    if g + 1 < G:
                        pair_scores(hp - 1, 1 - par, g + 1)
                    mix(hp - 1, 1 - par, g)

            stats(0)
            pe.wait_ge(s_xnlo, 2)
            projections(0, 0)
            for g in range(G):
                values(0, 0, g)
            pair_step(1, 1)
            with pe.Fori(2, HP, 2) as i:
                pair_step(i, 0)
                pair_step(i + 1, 1)
            pe.wait_ge(s_okcol, 1)
            pe.matmul(ps[0:1, 0, 0:1], ok_col[:, 0:1], ones[:, 0:1], start=True, stop=True).then_inc(s_okmm, 1)
            for g in range(G):
                pair_scores(HP - 1, 1, g)
                mix(HP - 1, 1, g)

            def general():
                with pe.Fori(0, HP) as hp:
                    pe.wait_ge(s_gw, 16 * hp + 16)
                    pe.wait_ge(s_gdone, hp + 1)
                    for mat in range(MATS):
                        pe.wait_ge(s_gread, 4 * hp + mat + 1)
                        for c in range(2):
                            for j in range(2):
                                for m in range(DC):
                                    w = wraw[0][:, (mat * DC + m) * P:(mat * DC + m + 1) * P]
                                    last = pe.matmul(ps[:, 2 * c + j, 0:GT], w, half(gx, c, (m,))[:, j, :],
                                                     start=(m == 0), stop=(m == DC - 1))
                        last.then_inc(s_gproj, 1)
                    with pe.Fori(0, T) as d:
                        pe.wait_ge(s_gterm, T * hp + d + 1)
                        for c in range(2):
                            for j in range(2):
                                last = pe.matmul(ps[:, 2 * c + j, 0:GT], head_sum[:], half(gprod, c)[:, j, :],
                                                 start=True, stop=True)
                        last.then_inc(s_gbc, 1)

            pe.wait_ge(s_ok, 1)
            in_range = pe.value_load(ok_sum[0:1, 0:1], min_val=0, max_val=P)
            with pe.If(in_range < P):
                general()

            pe.wait_ge(s_wo, 16)
            for c in range(2):
                pe.wait_ge(s_o, 4 * HP - 2 + 2 * c)
                if c == 0:
                    pe.wait_ge(s_way, 1)
                for m in range(DC):
                    if c == 1 and m == 0:
                        pe.wait_ge(s_p, 4 * HP)
                    for j in range(2):
                        for a in range(HP):
                            last = pe.matmul(ps[:, 4 * c + 2 * m + j, 0:GT], wo[:, a, m * P:(m + 1) * P],
                                             half(oT, c, (a,))[:, j, :], start=(a == 0), stop=(a == HP - 1))
                    last.then_inc(s_womm, 1)
            stats(1)

            pe.wait_ge(s_xnlo, 4)
            pe.wait_ge(s_wgs, 2)
            for r in range(RT):
                t0 = min(r * P, TOK - P)
                t = slice(t0, t0 + P)
                dst = ps[:, 0, r * E:(r + 1) * E]
                for m in range(DC):
                    pe.matmul(dst, xnlo[:, m, t], wghi[:, m, :], start=(m == 0), stop=False)
                    pe.matmul(dst, xnhi[:, m, t], wglo[:, m, :], start=False, stop=False)
                    last = pe.matmul(dst, xnhi[:, m, t], wghi[:, m, :], start=False, stop=(m == DC - 1))
            last.then_inc(s_lgmm, 1)

            def up(e, par, c):
                if c == 0:
                    pe.wait_ge(s_f1lo, e + 1)
                for j in range(FC):
                    n = 8 * e + 4 * c + j
                    if not (early(e, 1) and c == 0 and j < 2):
                        pe.wait_ge(s_relu, n - 1)
                    pairs = [(f1hi[par][:, m, j * P:(j + 1) * P], f1lo[par][:, m, j * P:(j + 1) * P],
                              [half(xnhi, c, (m,))[:, i, :] for i in range(2)],
                              [half(xnlo, c, (m,))[:, i, :] for i in range(2)]) for m in range(DC)]
                    three(pe, [ps[:, 2 * (j % 2) + i, 0:GT] for i in range(2)], pairs).then_inc(s_w1mm, 1)

            def down(e, par, c):
                if c == 0:
                    pe.wait_ge(s_f2lo, e + 1)
                pe.wait_ge(s_h1lo, 8 * e + 4 * c + 4)
                for m in range(DC):
                    if not (early(e, 1) and c == 0):
                        pe.wait_ge(s_comb, 4 * e + 2 * c + m - 1)
                    pairs = [(f2hi[par][:, j, m * P:(m + 1) * P], f2lo[par][:, j, m * P:(m + 1) * P],
                              [banks(h1hi[:, c, j, :])[:, i, :] for i in range(2)],
                              [banks(h1lo[:, c, j, :])[:, i, :] for i in range(2)]) for j in range(FC)]
                    three(pe, [ps[:, 4 + 2 * m + i, 0:GT] for i in range(2)], pairs).then_inc(s_w2mm, 1)

            def expert_step(e, par):
                for c in range(2):
                    down(e, par, c)
                    up(e + 1, 1 - par, c)

            pe.wait_ge(s_prob, 1)
            up(0, 0, 0)
            up(0, 0, 1)
            pe.wait_ge(s_sc, 1)
            for r in range(RT):
                last = pe.transpose(ps[0:E, 4 + r // 4, (r % 4) * P:(r % 4 + 1) * P], sc[:, r, :], ident[:])
            last.then_inc(s_sctmm, 1)
            pe.wait_ge(s_sct, 1)
            expert_step(0, 0)
            with pe.Fori(1, E - 1, 2) as i:
                expert_step(i, 1)
                expert_step(i + 1, 0)
            for c in range(2):
                down(E - 1, 1, c)

        @block.scalar
        def _(act):
            act.wait_ge(s_wr, 32)
            for c in range(2):
                for m in range(DC):
                    act.wait_ge(s_emb_mm, 2 * c + m + 1)
                    act.activation(
                        hT[:, m, c * HALF:(c + 1) * HALF].rearrange("p (b t) -> p b t", t=T)[:, :, 0:NP],
                        ps[:, 4 * c + m, 0:HB * NP].rearrange("p (b t) -> p b t", t=NP),
                        ACT.Identity, bias=btok[:, m:m + 1]).then_inc(s_emb, 1)

            def stats(k):
                for c in range(2):
                    n = 2 * k + c
                    act.wait_ge(s_xc, n + 1)
                    act.activation(sq[:, c], xc[:, c], ACT.Square).then_inc(s_sq, 1)
                for c in range(2):
                    n = 2 * k + c
                    act.wait_ge(s_var, n + 1)
                    act.activation(banks(std[:, c, :]), slot(2 * c + 1), ACT.Sqrt, bias=eps[:]).then_inc(s_std, 1)
                for c in range(2):
                    n = 2 * k + c
                    act.wait_ge(s_xn, n + 1)
                    act.activation(xnhi[:, :, c * HALF:(c + 1) * HALF], xc[:, c], ACT.Copy).then_inc(s_xnhi, 1)

            def split_pair(hp, par, wload):
                act.wait_ge(s_wload[par], wload)
                if not early(hp, 2):
                    act.wait_ge(s_vmm, 4 * hp - 4)
                act.activation(whi[par][:].rearrange("p a b n -> p (a b n)"), wraw[par][:, 0:WA], ACT.Copy)
                act.activation(bneg[par][:], wraw[par][:, WA:WA + 1], ACT.Copy, scale=-1.0).then_inc(s_whi, 1)

            def evacuate(hp, par):
                act.wait_ge(s_whi, hp + 1)
                for c in range(2):
                    act.wait_ge(s_proj, 6 * hp + 1 + c)
                    if not early(hp, 1):
                        act.wait_ge(s_u, 2 * hp - 1 + c)
                    act.activation(half(e_g, c), slot(c), ACT.Exp, bias=bneg[par][:], scale=-1.0
                                   ).then_inc(s_exp, 1)
                for c in range(2):
                    act.wait_ge(s_exp, 2 * hp + 1 + c)
                    if not early(hp, 1):
                        act.wait_ge(s_scan, 2 * hp - 1 + c)
                    tok = slice(c * HALF, (c + 1) * HALF)
                    act.activation(u_g[:, tok].rearrange("p (b t) -> p b t", t=T)[:, :, 1:T],
                                   e_g[:, tok].rearrange("p (b t) -> p b t", t=T)[:, :, 1:T],
                                   ACT.Copy, bias=1.0).then_inc(s_u, 1)

            def evacuate_q(hp):
                for c in range(2):
                    act.wait_ge(s_proj, 6 * hp + 5 + c)
                    if not early(hp, 1):
                        act.wait_ge(s_qa, 2 * hp - 1 + c)
                    act.activation(half(qraw, c), slot(c), ACT.Copy).then_inc(s_qraw, 1)

            def evacuate_v(hp, par, g):
                act.wait_ge(s_vmm, 4 * hp + g + 1)
                if not early(hp, 2) and g == 0:
                    act.wait_ge(s_omm, 4 * hp - 4)
                act.activation(vb[par][0:T, GB * g:GB * (g + 1), :].rearrange("p b n -> p (b n)"), ps[0:T, 6, :], ACT.Copy).then_inc(s_v, 1)

            def evacuate_o(a, g):
                act.wait_ge(s_omm, 4 * a + g + 1)
                act.activation(oT[:, bass.ds(a, 1), g * GT:(g + 1) * GT], ps[:, 7:8, 0:GT], ACT.Copy).then_inc(s_o, 1)

            def pair_step(hp, par, wload, tail=False):
                evacuate(hp, par)
                if not tail:
                    split_pair(hp + 1, 1 - par, wload)
                evacuate_q(hp)
                for g in range(G):
                    evacuate_v(hp, par, g)
                    evacuate_o(hp - 1, g)

            stats(0)
            split_pair(0, 0, 16)
            evacuate(0, 0)
            split_pair(1, 1, 16)
            evacuate_q(0)
            for g in range(G):
                evacuate_v(0, 0, g)
            pair_step(1, 1, 32)
            with act.Fori(2, HP - 2, 2) as i:
                pair_step(i, 0, 8 * i + 16)
                pair_step(i + 1, 1, 8 * i + 32)
            pair_step(HP - 2, 0, 16 * (HP // 2))
            pair_step(HP - 1, 1, 0, tail=True)
            for g in range(G):
                evacuate_o(HP - 1, g)

            def general():
                with act.Fori(0, HP) as hp:
                    act.wait_ge(s_gw, 16 * hp + 16)
                    act.wait_ge(s_gdone, hp + 1)
                    act.activation(bneg[0][:], wraw[0][:, WA:WA + 1], ACT.Copy, scale=-1.0).then_inc(s_gset, 1)
                    act.wait_ge(s_gset, hp + 1)
                    act.wait_ge(s_gproj, 4 * hp + 1)
                    for c in range(2):
                        last = act.activation(half(ga, c), slot(c), ACT.Exp, bias=bneg[0][:], scale=-1.0)
                    last.then_inc(s_gread, 1)

            act.wait_ge(s_ok, 1)
            in_range = act.value_load(ok_sum[0:1, 0:1], min_val=0, max_val=P)
            with act.If(in_range < P):
                general()

            act.wait_ge(s_wg, 16)
            act.activation(wghi[:], wg[:], ACT.Copy).then_inc(s_wgs, 1)
            stats(1)

            def split_expert(e, par, fload):
                act.wait_ge(s_fload[par], fload)
                if not early(e, 2):
                    act.wait_ge(s_comb, 4 * e - 4)
                    act.wait_ge(s_w1mm, 8 * e - 8)
                act.activation(f1hi[par][:].rearrange("p a n -> p (a n)"), fraw[par][:, 0:WF], ACT.Copy).then_inc(s_f1hi, 1)
                if not early(e, 2):
                    act.wait_ge(s_w2mm, 4 * e - 4)
                act.activation(f2hi[par][:].rearrange("p a n -> p (a n)"), fraw[par][:, WF:2 * WF], ACT.Copy)
                act.activation(fbias[par][:], fraw[par][:, 2 * WF:FPACK], ACT.Copy).then_inc(s_f2hi, 1)

            def relu(e, par, c):
                act.wait_ge(s_f2hi, e + 1)
                for j in range(FC):
                    n = 8 * e + 4 * c + j
                    act.wait_ge(s_w1mm, n + 1)
                    if not (early(e, 1) and c == 0 and j < 2):
                        act.wait_ge(s_h1lo, n - 1)
                    act.activation(banks(hf[j % 2][:]), slot(j % 2), ACT.Relu, bias=fbias[par][:, j:j + 1]
                                   ).then_inc(s_relu, 1)

            def expert_step(e, par, fload):
                split_expert(e + 1, 1 - par, fload)
                for c in range(2):
                    relu(e + 1, 1 - par, c)

            split_expert(0, 0, 16)
            act.wait_ge(s_prob, 1)
            act.activation(pr[:], lg[:], ACT.Exp).then_inc(s_exps, 1)
            relu(0, 0, 0)
            relu(0, 0, 1)
            act.wait_ge(s_sctmm, 1)
            act.activation(banks(scT[:, 0:1024]), ps[0:E, 4:6, 0:512], ACT.Copy)
            act.activation(scT[:, 1024:TOK], ps[0:E, 6, P - (TOK - 1024):P], ACT.Copy).then_inc(s_sct, 1)
            expert_step(0, 0, 16)
            with act.Fori(1, E - 1, 2) as i:
                expert_step(i, 1, 8 * i + 24)
                expert_step(i + 1, 0, 8 * i + 24)

        @block.vector
        def _(dve):
            links = [0]

            def link(ins):
                links[0] += 1
                ins.then_inc(s_link, 1)
                dve.wait_ge(s_link, links[0])

            dve.wait_ge(s_idx_in, 16)
            link(dve.tensor_copy(idx_f[:], idx_i[:]))
            link(dve.tensor_scalar(idx_n[:], idx_f[:], 0.0, float(VOCAB), ALU.is_lt, ALU.mult))
            link(dve.tensor_tensor(idx_f[:], idx_f[:], idx_n[:], ALU.add))
            dve.tensor_scalar(idx_u[:], idx_f[:], 0.0, float(VOCAB - 1), ALU.max, ALU.min).then_inc(s_idx, 1)
            dve.memset(u_ok[:], 1.0).then_inc(s_uok, 1)
            dve.wait_ge(s_gt_mm, 1)
            dve.tensor_copy(gT[:], ps[:, 7, :]).then_inc(s_gt, 1)
            for c in range(2):
                for m in range(DC):
                    dve.wait_ge(s_emb_mm, 4 + 2 * c + m + 1)
                    dve.tensor_copy(
                        hT[:, m, c * HALF:(c + 1) * HALF].rearrange("p (b t) -> p b t", t=T)[:, :, NP:T],
                        ps[:, 4 * c + 2 + m, 0:HB * NT].rearrange("p (b t) -> p b t", t=NT)).then_inc(s_txt, 1)

            def stats(k):
                for c in range(2):
                    n = 2 * k + c
                    dve.wait_ge(s_mean, n + 1)
                    if k == 0:
                        dve.wait_ge(s_emb, 2 * (c + 1))
                        dve.wait_ge(s_txt, 2 * (c + 1))
                    for m in range(DC):
                        last = dve.tensor_tensor(banks(xc[:, c, m, :]), half(hT, c, (m,)), slot(2 * c), ALU.subtract)
                    last.then_inc(s_xc, 1)
                for c in range(2):
                    n = 2 * k + c
                    dve.wait_ge(s_std, n + 1)
                    dve.reciprocal(rstd[:, c, :], std[:, c, :]).then_inc(s_rstd, 1)
                    dve.wait_ge(s_rstd, n + 1)
                    dve.wait_ge(s_sq, n + 1)
                    for m in range(DC):
                        last = dve.tensor_tensor(xc[:, c, m, :], xc[:, c, m, :], rstd[:, c, :], ALU.mult)
                    last.then_inc(s_xn, 1)
                for c in range(2):
                    n = 2 * k + c
                    dve.wait_ge(s_xnhi, n + 1)
                    tok = slice(c * HALF, (c + 1) * HALF)
                    dve.tensor_tensor(xnlo[:, :, tok], xc[:, c], xnhi[:, :, tok].bitcast(F32), ALU.subtract
                                      ).then_inc(s_xnlo, 1)

            def decay(hp, par):
                for c in range(2):
                    dve.wait_ge(s_u, 2 * hp + c + 1)
                    if not early(hp, 1):
                        dve.wait_ge(s_a, 4 * hp - 2 + 2 * c)
                    dve.tensor_tensor_scan(U[:, c * HALF:(c + 1) * HALF], u_g[:, c * HALF:(c + 1) * HALF], first[:],
                                           1.0, ALU.mult, ALU.add).then_inc(s_scan, 1)
                    dve.wait_ge(s_scan, 2 * hp + c + 1)
                    dve.wait_ge(s_proj, 6 * hp + 3 + c)
                    if c == 0 and not early(hp, 2):
                        dve.wait_ge(s_pmm, 4 * hp - 4)
                    dve.tensor_tensor(half(kU[par], c), slot(c), half(U, c), ALU.mult).then_inc(s_ku, 1)
                dve.wait_ge(s_uok, hp + 1)
                dve.scalar_tensor_tensor(u_ok[:], U[:].rearrange("p (b t) -> p b t", t=T)[:, :, T - 1], U_LIMIT,
                                         u_ok[:], ALU.is_le, ALU.mult).then_inc(s_uok, 1)

            def invert(hp, g):
                if not early(hp, 1):
                    dve.wait_ge(s_qa, 2 * hp - 1 + g // 2)
                dve.reciprocal(A[:, g * GT:(g + 1) * GT], U[:, g * GT:(g + 1) * GT]).then_inc(s_a, 1)

            def mask(a, g):
                dve.wait_ge(s_pmm, 4 * a + g + 1)
                if not (early(a, 1) and g < 2):
                    dve.wait_ge(s_omm, 4 * a + g - 1)
                dve.tensor_tensor(pb[g % 2][0:T].bitcast(U32), ps[0:T, 4:6, 0:GT].bitcast(U32), causal_bits[0:T],
                                  ALU.bitwise_and).then_inc(s_p, 1)

            def pair_step(hp, par):
                decay(hp, par)
                for g in range(G):
                    invert(hp, g)
                    mask(hp - 1, g)

            stats(0)
            dve.wait_ge(s_const, 6)
            dve.tensor_scalar(causal_bits[:].bitcast(I32), causal[:], -1.0, None, ALU.mult)
            dve.wait_ge(s_first, 1)
            decay(0, 0)
            for g in range(G):
                invert(0, g)
            pair_step(1, 1)
            with dve.Fori(2, HP, 2) as i:
                pair_step(i, 0)
                pair_step(i + 1, 1)
            dve.wait_ge(s_uok, HP + 1)
            dve.tensor_reduce(ok_col[:], u_ok[:], AX_X, ALU.min).then_inc(s_okcol, 1)
            dve.wait_ge(s_okmm, 1)
            dve.tensor_copy(ok_sum[:], ps[0:1, 0, 0:1]).then_inc(s_ok, 1)
            for g in range(G):
                mask(HP - 1, g)
            dve.wait_ge(s_ok, 1)

            def general():
                dve.wait_ge(s_o, 4 * HP)
                dve.wait_ge(s_qa, 2 * HP)
                dve.tensor_tensor(gx[:], xnhi[:].bitcast(F32), xnlo[:].bitcast(F32), ALU.add)
                dve.memset(head_sum[:], 0.0)
                dve.drain()
                dve.memset(head_sum[0:DK, 0:DK], 1.0)
                dve.memset(head_sum[DK:P, DK:P], 1.0).then_inc(s_gread, 1)
                dve.drain().then_inc(s_gdone, 1)

                def by_batch(t):
                    return t[:].rearrange("p (b t) -> p b t", t=T)

                with dve.Fori(0, HP) as hp:
                    for i, dst in ((KEY, gk[0]), (QUERY, gq), (VALUE, gv[0])):
                        dve.wait_ge(s_gproj, 4 * hp + i + 1)
                        for c in range(2):
                            last = dve.tensor_copy(half(dst, c), slot(c))
                        last.then_inc(s_gread, 1)
                    dve.tensor_scalar(ga[:], ga[:], 1.0, None, ALU.add)
                    dve.drain()
                    dve.reciprocal(ga[:], ga[:])
                    dve.memset(gsum[:], 0.0)
                    dve.drain()
                    with dve.Fori(0, T, 2) as d:
                        for i in range(2):
                            dve.tensor_tensor(gprod[:], gq[:], gk[i][:], ALU.mult).then_inc(s_gterm, 1)
                            dve.tensor_tensor(by_batch(gk[1 - i])[:, :, 1:T], by_batch(ga)[:, :, 1:T],
                                              by_batch(gk[i])[:, :, 0:T - 1], ALU.mult)
                            dve.memset(by_batch(gk[1 - i])[:, :, 0:1], 0.0)
                            dve.tensor_copy(by_batch(gv[1 - i])[:, :, 1:T], by_batch(gv[i])[:, :, 0:T - 1])
                            dve.memset(by_batch(gv[1 - i])[:, :, 0:1], 0.0)
                            dve.wait_ge(s_gbc, T * hp + d + i + 1)
                            for c in range(2):
                                dve.tensor_tensor(half(gprod, c), slot(c), half(gv[i], c), ALU.mult)
                            dve.drain()
                            dve.tensor_tensor(gsum[:], gsum[:], gprod[:], ALU.add)
                            dve.drain()
                    dve.tensor_copy(oT[:, bass.ds(hp, 1), :], gsum[:].unsqueeze(1))
                    dve.drain().then_inc(s_gdone, 1)

            in_range = dve.value_load(ok_sum[0:1, 0:1], min_val=0, max_val=P)
            with dve.If(in_range < P):
                general()
            dve.drain().then_inc(s_way, 1)

            for c in range(2):
                for m in range(DC):
                    dve.wait_ge(s_womm, 2 * c + m + 1)
                    dve.tensor_tensor(half(hT, c, (m,)), half(hT, c, (m,)), slot(2 * c + m), ALU.add).then_inc(s_h2, 1)
            dve.wait_ge(s_wgs, 1)
            dve.tensor_tensor(wglo[:], wg[:], wghi[:].bitcast(F32), ALU.subtract).then_inc(s_wgs, 1)
            dve.wait_ge(s_h2, 4)
            stats(1)

            def wide(t):
                return t.unsqueeze(2).to_broadcast([P, RT, E])

            logits = ps[:, 0, 0:RT * E].rearrange("p (r e) -> p r e", e=E)
            dve.wait_ge(s_lgmm, 1)
            link(dve.tensor_reduce(rs[:, 0, :], logits, AX_X, ALU.max))
            dve.tensor_tensor(lg[:], logits, wide(rs[:, 0, :]), ALU.subtract).then_inc(s_prob, 1)
            dve.wait_ge(s_exps, 1)
            link(dve.tensor_reduce(rs[:, 1, :], pr[:], AX_X, ALU.add))
            link(dve.reciprocal(rs[:, 1, :], rs[:, 1, :]))
            link(dve.tensor_tensor(pr[:], pr[:], wide(rs[:, 1, :]), ALU.mult))
            for r in range(RT):
                last = dve.max(top[:, r, :], pr[:, r, :])
            link(last)
            for r in range(RT):
                last = dve.max_index(topi[:, r, :], top[:, r, :], pr[:, r, :])
            link(last)
            link(dve.tensor_copy(topf[:], topi[:]))
            link(dve.tensor_tensor(rs[:, 2, :], top[:, :, 0], top[:, :, 1], ALU.add))
            link(dve.reciprocal(rs[:, 2, :], rs[:, 2, :]))
            for i in range(2):
                link(dve.tensor_tensor(rs[:, 3, :], top[:, :, i], rs[:, 2, :], ALU.mult))
                link(dve.tensor_tensor(pick[:, i], iota_e[:], wide(topf[:, :, i]), ALU.is_equal))
                link(dve.tensor_tensor(pick[:, i], pick[:, i], wide(rs[:, 3, :]), ALU.mult))

            def split_hidden(e, c):
                for j in range(FC):
                    n = 8 * e + 4 * c + j
                    dve.wait_ge(s_relu, n + 1)
                    if j == 0 and not early(e, 1):
                        dve.wait_ge(s_w2mm, 4 * e + 2 * c - 2)
                    dve.tensor_copy(h1hi[:, c, j, :], hf[j % 2][:]).then_inc(s_h1hi, 1)
                    dve.wait_ge(s_h1hi, n + 1)
                    dve.tensor_tensor(h1lo[:, c, j, :], hf[j % 2][:], h1hi[:, c, j, :].bitcast(F32), ALU.subtract
                                      ).then_inc(s_h1lo, 1)

            def combine(e, par, c):
                for m in range(DC):
                    dve.wait_ge(s_w2mm, 4 * e + 2 * c + m + 1)
                    if not (early(e, 1) and c == 0):
                        dve.wait_ge(s_acc, 4 * e + 2 * c + m - 1)
                    dve.scalar_tensor_tensor(banks(ytmp[m][:]), slot(2 + m), fbias[par][:, FC + m:FC + m + 1],
                                             half(scb[par], c), ALU.add, ALU.mult).then_inc(s_comb, 1)

            def expert_step(e, par, scb_count):
                dve.wait_ge(s_scb[par], scb_count)
                for c in range(2):
                    combine(e, par, c)
                    split_hidden(e + 1, c)

            split_hidden(0, 0)
            dve.tensor_tensor(sc[:], pick[:, 0], pick[:, 1], ALU.add).then_inc(s_sc, 1)
            split_hidden(0, 1)
            expert_step(0, 0, 16)
            with dve.Fori(1, E - 1, 2) as i:
                expert_step(i, 1, 8 * i + 8)
                expert_step(i + 1, 0, 8 * i + 24)
            dve.wait_ge(s_scb[1], 16 * (E // 2))
            for c in range(2):
                combine(E - 1, 1, c)

        @block.gpsimd
        def _(pool):
            pool.wait_ge(s_idx, 1)
            for g in range(G):
                if g:
                    pool.wait_ge(s_gath, 16 * g)
                pool.indirect_dma_start(out=gath[:, g, :], out_offset=None, in_=w_l,
                                        in_offset=bass.IndirectOffsetOnAxis(ap=idx_u[:, g:g + 1], axis=0),
                                        bounds_check=VOCAB - 1).then_inc(s_gath, 16)
            pool.memset(ident[:], 0.0).then_inc(s_const, 1)
            pool.memset(mean_w[:], 1.0 / D).then_inc(s_const, 1)
            pool.memset(eps[:], LN_EPS).then_inc(s_const, 1)
            pool.memset(ones[:], 1.0).then_inc(s_const, 1)
            pool.wait_ge(s_const, 4)
            pool.affine_select(out=ident[:], in_=ident[:], compare_op=ALU.not_equal, fill=1.0, base=0,
                               pattern=[[-1, P]], channel_multiplier=1).then_inc(s_const, 1)
            pool.iota(iota_e[:], pattern=[[0, RT], [1, E]], base=0, channel_multiplier=0,
                      allow_small_or_imprecise_dtypes=True)
            pool.memset(first[:], 0.0)
            pool.memset(causal[:], 1.0).then_inc(s_link2, 1)
            pool.wait_ge(s_link2, 1)
            pool.memset(first[:].rearrange("p (b t) -> p b t", t=T)[:, :, 0:1], 1.0)
            keep = causal[:].rearrange("p h (b t) -> p (h b) t", t=T)
            pool.affine_select(out=keep, in_=keep, compare_op=ALU.is_ge, fill=0.0, base=0,
                               pattern=[[0, 2 * GB], [1, T]], channel_multiplier=-1).then_inc(s_const, 1)

            def split_pair(hp, par):
                pool.wait_ge(s_whi, hp + 1)
                pool.tensor_tensor(wlo[par][:].rearrange("p a b n -> p (a b n)"), wraw[par][:, 0:WA],
                                   whi[par][:].bitcast(F32).rearrange("p a b n -> p (a b n)"), ALU.subtract
                                   ).then_inc(s_wlo, 1)

            def scale_q(hp, par):
                for c in range(2):
                    pool.wait_ge(s_qraw, 2 * hp + 1 + c)
                    pool.wait_ge(s_a, 4 * hp + 2 + 2 * c)
                    if c == 0 and not early(hp, 2):
                        pool.wait_ge(s_pmm, 4 * hp - 4)
                    tok = slice(c * HALF, (c + 1) * HALF)
                    pool.tensor_tensor(qA[par][:, tok], qraw[:, tok], A[:, tok], ALU.mult).then_inc(s_qa, 1)

            def pair_step(hp, par, tail=False):
                if not tail:
                    split_pair(hp + 1, 1 - par)
                scale_q(hp, par)

            split_pair(0, 0)
            pool.wait_ge(s_xnlo, 2)
            pool.memset(u_g[:].rearrange("p (b t) -> p b t", t=T)[:, :, 0:1], 0.0).then_inc(s_first, 1)
            split_pair(1, 1)
            scale_q(0, 0)
            pair_step(1, 1)
            with pool.Fori(2, HP - 2, 2) as i:
                pair_step(i, 0)
                pair_step(i + 1, 1)
            pair_step(HP - 2, 0)
            pair_step(HP - 1, 1, tail=True)

            def split_expert(e, par):
                pool.wait_ge(s_f1hi, e + 1)
                pool.tensor_tensor(f1lo[par][:].rearrange("p a n -> p (a n)"), fraw[par][:, 0:WF],
                                   f1hi[par][:].bitcast(F32).rearrange("p a n -> p (a n)"), ALU.subtract
                                   ).then_inc(s_f1lo, 1)
                pool.wait_ge(s_f2hi, e + 1)
                pool.tensor_tensor(f2lo[par][:].rearrange("p a n -> p (a n)"), fraw[par][:, WF:2 * WF],
                                   f2hi[par][:].bitcast(F32).rearrange("p a n -> p (a n)"), ALU.subtract
                                   ).then_inc(s_f2lo, 1)

            def accumulate(e, c):
                for m in range(DC):
                    q = 4 * e + 2 * c + m
                    pool.wait_ge(s_comb, q + 1)
                    if not early(e, 1):
                        pool.wait_ge(s_acc, q - 3)
                    pool.tensor_tensor(hT[:, m, c * HALF:(c + 1) * HALF], hT[:, m, c * HALF:(c + 1) * HALF],
                                       ytmp[m][:], ALU.add).then_inc(s_acc, 1)

            def expert_step(e, par):
                split_expert(e + 1, 1 - par)
                for c in range(2):
                    accumulate(e, c)

            split_expert(0, 0)
            expert_step(0, 0)
            with pool.Fori(1, E - 1, 2) as i:
                expert_step(i, 1)
                expert_step(i + 1, 0)
            for c in range(2):
                accumulate(E - 1, c)


def kernel(x, x_txt, L0_tok_W, L0_tok_b, L0_txt_weight_l, L0_txt_weight_r, L0_attn_W_q, L0_attn_W_k, L0_attn_W_v,
           L0_attn_W_gate, L0_attn_b_gate, L0_attn_W_o, L0_ffn_Wg, L0_ffn_W1, L0_ffn_b1, L0_ffn_W2, L0_ffn_b2):
    import concourse.bacc as bacc
    from concourse.bass_utils import run_bass_kernel_spmd as run

    a = np.asarray
    c = np.ascontiguousarray
    runs = a(x).transpose(0, 2, 1, 3).reshape(2, HB * NP, PC, P)

    def rows(w, n):
        w = a(w)
        return w.reshape(n, P, w.shape[-1]).transpose(1, 0, 2)

    mats = [a(w).reshape(DC, P, HP, P).transpose(2, 1, 0, 3).reshape(HP, P, DC * P)
            for w in (L0_attn_W_gate, L0_attn_W_k, L0_attn_W_q, L0_attn_W_v)]
    arrays = {
        "x_idx": c(a(x_txt).reshape(G, P).T),
        "patches": c(runs.transpose(0, 3, 2, 1)),
        "w_tok": c(rows(a(L0_tok_W).T, PC)),
        "b_tok": c(a(L0_tok_b).reshape(DC, P).T),
        "w_l": c(a(L0_txt_weight_l)),
        "w_r": c(a(L0_txt_weight_r)),
        "w_attn": np.concatenate([*mats, a(L0_attn_b_gate).reshape(HP, P, 1)], axis=2),
        "w_o": c(rows(L0_attn_W_o, HP)),
        "w_gate": c(rows(L0_ffn_Wg, DC)),
        "w_ffn": np.concatenate([
            a(L0_ffn_W1).reshape(E, DC, P, FH).transpose(0, 2, 1, 3).reshape(E, P, WF),
            a(L0_ffn_W2).reshape(E, FC, P, D).transpose(0, 2, 1, 3).reshape(E, P, WF),
            a(L0_ffn_b1).reshape(E, FC, P).transpose(0, 2, 1),
            a(L0_ffn_b2).reshape(E, DC, P).transpose(0, 2, 1)], axis=2),
    }
    nc = bacc.Bacc("TRN2", target_bir_lowering=False, num_devices=1)
    ins = {n: nc.dram_tensor(n, v.shape, mybir.dt.from_np(v.dtype), kind="ExternalInput").ap()
           for n, v in arrays.items()}
    out = nc.dram_tensor("out", (P, DC, TOK), F32, kind="ExternalOutput").ap()
    scores = nc.dram_tensor("scores", (E, TOK), F32, kind="Internal").ap()
    build(nc, **ins, out=out, scores_dram=scores)
    got = run(nc, [arrays], core_ids=[0]).results[0]["out"]
    return got.transpose(1, 0, 2).reshape(D, B, T).transpose(1, 2, 0)
```

```python
from contextlib import ExitStack

import numpy as np

import concourse.bass as bass
from concourse import mybir

F32 = mybir.dt.float32
F32R = mybir.dt.float32r
I32 = mybir.dt.int32
U32 = mybir.dt.uint32
ALU = mybir.AluOpType
ACT = mybir.ActivationFunctionType
AX_X = mybir.AxisListType.X

P = 128
B, NP, NT = 16, 36, 32
T = NP + NT
TOK = B * T
D, PD = 256, 768
KE = 128
VOCAB = 32000
H, DK = 16, 64
HP = H // 2
E, FH = 8, 512
DC, PC, FC = D // P, PD // P, FH // P
HALF = TOK // 2
GB = 4
G = B // GB
GT = GB * T
HB = B // 2
U_LIMIT = 1e25
LN_EPS = 1e-5
MATS = 4
GATE, KEY, QUERY, VALUE = range(MATS)
WA = MATS * DC * P
WF = DC * FH
EP = 3
RT = -(-TOK // P)
DUP = RT * P - TOK
PICKS = 2
A = PICKS * RT
NB = (PICKS * TOK - E) // P + E
BN = -(-TOK // P)
XQ = -(-HALF // P)
XTAIL = HALF - (XQ - 1) * P
EARLY_W = 3


def build(nc, x_idx, patches, w_tok, b_tok, w_l, w_r, w_attn, w_o, w_gate, w_ffn, b_ffn, out, xrows):
    with ExitStack() as ctx:
        def sem(name):
            return ctx.enter_context(nc.semaphore(name))

        cursor = [16512]

        def sb(name, shape, dt=F32, at=None):
            c = cursor if at is None else at
            t = nc.alloc_sbuf_tensor_at(name, shape, dt, offset=c[0])
            c[0] += -(-int(np.prod(shape[1:])) * 4 // 32) * 32
            assert c[0] <= nc.sbuf_usable_end
            return t

        hT = sb("hT", [P, DC, TOK])
        xnhi = sb("xnhi", [P, DC, TOK], F32R)
        xnlo = sb("xnlo", [P, DC, TOK], F32R)
        start_o = cursor[0]
        oT = sb("oT", [P, HP, TOK])
        wo = sb("wo", [P, HP, D])
        end_o = cursor[0]
        causal = sb("causal", [P, 2, GT])
        causal_bits = sb("causal_bits", [P, 2, GT], U32)
        first = sb("first", [P, HALF])
        ident = sb("ident", [P, P])
        mean_w = sb("mean_w", [P, P])
        ones = sb("ones", [P, 1])
        eps = sb("eps", [P, 1])
        warm = sb("warm", [P, 1])
        btok = sb("btok", [P, DC])
        u_ok = sb("u_ok", [P, B])
        ok_col = sb("ok_col", [P, 1])
        ok_sum = sb("ok_sum", [1, 1], I32)
        wg = sb("wg", [P, DC, E])
        tri = sb("tri", [P, P])
        expert_no = sb("expert_no", [P, PICKS, RT, E])
        seg = sb("seg", [P, E, A])
        steps = sb("steps", [P, E, BN - 1])
        block_start = sb("block_start", [P, NB])
        block_no = sb("block_no", [P, NB, E])
        place = sb("place", [P, P])
        row_no = sb("row_no", [P, PICKS, RT])
        ones_e = sb("ones_e", [P, E])
        spare_no = sb("spare_no", [P, 1])
        lgT = sb("lgT", [E, TOK])
        lg = sb("lg", [P, RT, E])
        pr = sb("pr", [P, RT, E])
        top = sb("top", [P, RT, 8])
        topi = sb("topi", [P, RT, 8], U32)
        topf = sb("topf", [P, RT, 8])
        rs = sb("rs", [P, 3, RT])
        idx_i = sb("idx_i", [P, G], I32)
        idx_f = sb("idx_f", [P, G])
        idx_n = sb("idx_n", [P, G])
        idx_u = sb("idx_u", [P, G], U32)

        start_w = cursor[0]
        pt = sb("pt", [P, 2, PC, HB * NP])
        wtok = sb("wtok", [P, PC, D])
        gath = sb("gath", [P, G, KE])
        gT = sb("gT", [P, B * NT])
        wr = sb("wr", [P, D])

        start = cursor[0]
        e_g = sb("e_g", [P, TOK])
        u_g = sb("u_g", [P, TOK])
        U = sb("U", [P, TOK])
        invU = sb("invU", [P, TOK])
        qraw = sb("qraw", [P, TOK])
        kU = [sb(f"kU{i}", [P, TOK]) for i in range(2)]
        ln_end = cursor[0]
        qA = [sb(f"qA{i}", [P, TOK]) for i in range(2)]
        vb = [sb(f"vb{i}", [P, B, P]) for i in range(2)]
        pb = [sb(f"pb{i}", [P, 2, GT]) for i in range(2)]
        pb_end = cursor[0]
        wraw = [sb(f"wraw{i}", [P, WA + 1]) for i in range(2)]
        bneg = [sb(f"bneg{i}", [P, 1]) for i in range(2)]
        whi = [sb(f"whi{i}", [P, MATS, DC, P], F32R) for i in range(2)]
        wlo = [sb(f"wlo{i}", [P, MATS, DC, P], F32R) for i in range(2)]
        attn_end = cursor[0]
        over = [start_w]
        w1 = sb("w1", [P, E, 2 * WF], at=over)
        assert EARLY_W * 2 * WF * 4 <= start - start_w
        bias = sb("bias", [P, E, FH + D], at=over)
        xrow = sb("xrow", [P, 2, XQ, D], at=over)
        hrow = sb("hrow", [P, 2, XQ, D], at=over)
        cursor[0] = max(cursor[0], over[0])
        over = [start_o]
        share = sb("share", [P, PICKS, RT], at=over)
        share_hi = sb("share_hi", [P, PICKS, RT], F32R, at=over)
        share_lo = sb("share_lo", [P, PICKS, RT], F32R, at=over)
        pick = sb("pick", [P, PICKS, RT, E], at=over)
        total = sb("total", [P, E, A], at=over)
        upto = sb("upto", [P, E, A], at=over)
        more = sb("more", [P, E, BN - 1], at=over)
        blocks = sb("blocks", [P, 3, E], at=over)
        pos_e = sb("pos_e", [P, A, E], at=over)
        pos = sb("pos", [P, A], at=over)
        pos_i = sb("pos_i", [P, A], I32, at=over)
        place_of = sb("place_of", [P, A], at=over)
        border = sb("border", [P, A], at=over)
        in_block = sb("in_block", [P, A, NB], at=over)
        at_place = sb("at_place", [P, A, P], F32R, at=over)
        entry = sb("entry", [P, A, 3, NB], F32R, at=over)
        table = sb("table", [P, 3, NB], at=over)
        tab = sb("tab", [P, 1, NB], at=over)
        shares = sb("shares", [P, NB], at=over)
        gather_u = sb("gather_u", [P, NB], U32, at=over)
        scatter_u = sb("scatter_u", [P, NB], U32, at=over)
        passed = sb("passed", [P, NB, E], at=over)
        owner = sb("owner", [P, NB], at=over)
        owner_i = sb("owner_i", [P, NB], I32, at=over)
        xg = [sb(f"xg{i}", [P, D], at=over) for i in range(2)]
        xt = [sb(f"xt{i}", [P, D], at=over) for i in range(2)]
        hb = [sb(f"hb{i}", [P, FH], at=over) for i in range(2)]
        hr = [sb(f"hr{i}", [P, FH], at=over) for i in range(2)]
        yb = [sb(f"yb{i}", [P, D], at=over) for i in range(2)]
        ys = [sb(f"ys{i}", [P, D], at=over) for i in range(2)]
        assert over[0] <= end_o, (over[0], end_o)
        at_xc = cursor[0]
        xc = sb("xc", [P, 2, DC, HALF])
        std = sb("std", [P, 2, HALF])
        vT = nc.alloc_sbuf_tensor_at("vT", [P, TOK], F32, offset=at_xc)
        over = [start]
        gx = sb("gx", [P, DC, TOK], at=over)
        gq, ga, gsum, gprod = (sb(n, [P, TOK], at=over) for n in ("gq", "ga", "gsum", "gprod"))
        gk = [sb(f"gk{i}", [P, TOK], at=over) for i in range(2)]
        gv = [sb(f"gv{i}", [P, TOK], at=over) for i in range(2)]
        head_sum = sb("head_sum", [P, P], at=over)
        assert over[0] <= pb_end
        assert cursor[0] <= nc.sbuf_usable_end, cursor[0]

        ps = ctx.enter_context(nc.psum_tensor("ps", [P, 8, 512], F32))

        def slot(k, n=GT):
            return ps[:, 2 * k:2 * k + 2, 0:n]

        def half(t, c, lead=()):
            return t[(slice(None),) + lead + (slice(c * HALF, (c + 1) * HALF),)].rearrange(
                "p (j n) -> p j n", j=2)

        def banks(t):
            return t.rearrange("p (j n) -> p j n", j=2)

        def squares(c):
            return oT[:, DC * c:DC * (c + 1), 0:HALF]

        def rstd(c):
            return oT[:, 2 * DC + c, 0:HALF]

        s_idx_in, s_idx, s_gath = sem("s_idx_in"), sem("s_idx"), sem("s_gath")
        s_emb_in = [sem(f"s_emb_in{i}") for i in range(EP + 1)]
        s_wr, s_wo, s_wg = sem("s_wr"), sem("s_wo"), sem("s_wg")
        s_const = sem("s_const")
        s_gt_mm, s_gt = sem("s_gt_mm"), sem("s_gt")
        s_patch_mm, s_text_mm, s_emb, s_txt = sem("s_patch_mm"), sem("s_text_mm"), sem("s_emb"), sem("s_txt")
        s_mean, s_xc, s_sq, s_var, s_std = sem("s_mean"), sem("s_xc"), sem("s_sq"), sem("s_var"), sem("s_std")
        s_rstd, s_xn, s_xnhi, s_xnlo = sem("s_rstd"), sem("s_xn"), sem("s_xnhi"), sem("s_xnlo")
        s_wload = [sem("s_wload0"), sem("s_wload1")]
        s_whi, s_wlo = sem("s_whi"), sem("s_wlo")
        s_proj, s_exp, s_u, s_scan, s_ku = sem("s_proj"), sem("s_exp"), sem("s_u"), sem("s_scan"), sem("s_ku")
        s_uok, s_qraw, s_a, s_qa = sem("s_uok"), sem("s_qraw"), sem("s_a"), sem("s_qa")
        s_vt, s_vmm, s_v, s_pmm, s_p, s_omm, s_o = (sem(n) for n in ("s_vt", "s_vmm", "s_v", "s_pmm", "s_p", "s_omm", "s_o"))
        s_okcol, s_okmm, s_ok, s_way = sem("s_okcol"), sem("s_okmm"), sem("s_ok"), sem("s_way")
        s_womm, s_h2 = sem("s_womm"), sem("s_h2")
        s_rows_mm, s_rows, s_xrows, s_hrows = sem("s_rows_mm"), sem("s_rows"), sem("s_xrows"), sem("s_hrows")
        s_lgmm, s_lgt, s_lgtok, s_prob, s_exps = (sem(n) for n in ("s_lgmm", "s_lgt", "s_lgtok", "s_prob", "s_exps"))
        s_pick, s_count, s_share, s_off, s_place, s_entry, s_tabmm, s_owner, s_tab = (
            sem(n) for n in ("s_pick", "s_count", "s_share", "s_off", "s_place", "s_entry", "s_tabmm", "s_owner", "s_tab"))
        s_experts, s_bias = sem("s_experts"), sem("s_bias")
        s_gx = [sem("s_gx0"), sem("s_gx1")]
        s_tx, s_xt, s_up, s_hb, s_th, s_hr, s_dn, s_yb, s_ys, s_added = (
            sem(n) for n in ("s_tx", "s_xt", "s_up", "s_hb", "s_th", "s_hr", "s_dn", "s_yb", "s_ys", "s_added"))
        s_gw, s_gset, s_gproj, s_gread, s_gterm, s_gbc, s_gdone = (
            sem(n) for n in ("s_gw", "s_gset", "s_gproj", "s_gread", "s_gterm", "s_gbc", "s_gdone"))
        s_link, s_link2, s_first = sem("s_link"), sem("s_link2"), sem("s_first")

        block = ctx.enter_context(nc.Block())

        def early(n, count):
            return isinstance(n, int) and n < count

        def proj_done(hp, mat, c):
            return MATS * c + mat + 1 if early(hp, 1) else 2 * MATS * hp + 2 * mat + c + 1

        def proj_slot(hp, mat, c):
            return {GATE: 0, KEY: 1, QUERY: 3, VALUE: 2}[mat] if early(hp, 1) else c

        @block.sync
        def _(sp):
            sp.dma_start(idx_i[:], x_idx).then_inc(s_idx_in, 16)
            for i in range(EP):
                k = slice(i * PC // EP, (i + 1) * PC // EP)
                sp.dma_start(wtok[:, k], w_tok[:, k]).then_inc(s_emb_in[i], 16)
                sp.dma_start(pt[:, 0, k], patches[0, :, k]).then_inc(s_emb_in[i], 16)
                if i == 0:
                    sp.dma_start(wr[:], w_r).then_inc(s_wr, 16)
                    sp.dma_start(btok[:], b_tok).then_inc(s_wr, 16)
            sp.dma_start(pt[:, 1], patches[1]).then_inc(s_emb_in[EP], 16)
            for hp in range(HP):
                if hp >= 2:
                    sp.wait_ge(s_wlo, hp - 1)
                sp.dma_start(wraw[hp % 2][:], w_attn[hp]).then_inc(s_wload[hp % 2], 16)
                if hp == 1:
                    sp.dma_start(wo[:], w_o).then_inc(s_wo, 16)
                    sp.dma_start(wg[:], w_gate).then_inc(s_wg, 16)
            for e in range(EARLY_W):
                sp.dma_start(w1[:, e], w_ffn[e]).then_inc(s_experts, 16)
            sp.wait_ge(s_ok, 1)
            in_range = sp.value_load(ok_sum[0:1, 0:1], min_val=0, max_val=P)
            with sp.If(in_range < P):
                with sp.Fori(0, HP) as hp:
                    sp.wait_ge(s_gdone, hp + 1)
                    sp.dma_start(wraw[0][:], w_attn[bass.ds(hp, 1)].rearrange("o p n -> (o p) n")
                                 ).then_inc(s_gw, 16)
            sp.wait_ge(s_way, 1)
            sp.wait_ge(s_o, 4 * HP)
            sp.dma_start(w1[:, EARLY_W:], w_ffn[EARLY_W:].rearrange("e p n -> p e n")).then_inc(s_experts, 16)
            sp.dma_start(bias[:], b_ffn.to_broadcast([P, E * (FH + D)])).then_inc(s_bias, 16)

            def rows(dram, t, c, done):
                at = c * HALF
                sp.dma_start(dram[at:at + (XQ - 1) * P].rearrange("(q p) d -> p q d", p=P), t[:, c, 0:XQ - 1]
                             ).then_inc(done, 16)
                sp.dma_start(dram[at + (XQ - 1) * P:at + HALF], t[0:XTAIL, c, XQ - 1]).then_inc(done, 16)

            for n, (dram, t, c, done) in enumerate(((xrows, xrow, 0, s_xrows), (out, hrow, 0, s_hrows),
                                                    (out, hrow, 1, s_hrows), (xrows, xrow, 1, s_xrows))):
                sp.wait_ge(s_rows, n + 1)
                rows(dram, t, c, done)
            sp.dma_start(out[TOK:TOK + P], hrow[:, 0, 0]).then_inc(s_hrows, 16)
            sp.wait_ge(s_xrows, 64)
            sp.wait_ge(s_hrows, 80)
            sp.wait_ge(s_added, 16 * NB)

        def three(pe, outs, pairs):
            for n, dst in enumerate(outs):
                for i, (shi, slo, mhi, mlo) in enumerate(pairs):
                    pe.matmul(dst, slo, mhi[n], start=(i == 0), stop=False)
                    pe.matmul(dst, shi, mlo[n], start=False, stop=False)
                    last = pe.matmul(dst, shi, mhi[n], start=False, stop=(i == len(pairs) - 1))
            return last

        @block.tensor
        def _(pe):
            def embed_patches(c):
                for k in range(PC):
                    if c == 0 and k % (PC // EP) == 0:
                        pe.wait_ge(s_emb_in[k // (PC // EP)], 32)
                    if c == 1 and k == 0:
                        pe.wait_ge(s_emb_in[EP], 16)
                    for m in range(DC):
                        last = pe.matmul(ps[:, 4 * c + m, 0:HB * NP], wtok[:, k, m * P:(m + 1) * P],
                                         pt[:, c, k, :], start=(k == 0), stop=(k == PC - 1))
                last.then_inc(s_patch_mm, 1)

            def embed_text(c):
                if c == 0:
                    pe.wait_ge(s_const, 5)
                    pe.wait_ge(s_gath, 16 * G)
                    for g in range(G):
                        last = pe.transpose(ps[:, 7, g * P:(g + 1) * P], gath[:, g, :], ident[:])
                    last.then_inc(s_gt_mm, 1)
                    pe.wait_ge(s_gt, 1)
                    pe.wait_ge(s_wr, 32)
                for m in range(DC):
                    last = pe.matmul(ps[:, 4 * c + 2 + m, 0:HB * NT], wr[:, m * P:(m + 1) * P],
                                     gT[:, c * HB * NT:(c + 1) * HB * NT], start=True, stop=True)
                last.then_inc(s_text_mm, 1)

            def mean(k, c):
                if k == 0:
                    pe.wait_ge(s_emb, c + 1)
                    pe.wait_ge(s_txt, c + 1)
                else:
                    pe.wait_ge(s_h2, 2 * (c + 1))
                for j in range(2):
                    for m in range(DC):
                        last = pe.matmul(ps[:, 4 * c + j, 0:GT], mean_w[:], half(hT, c, (m,))[:, j, :],
                                         start=(m == 0), stop=(m == DC - 1))
                last.then_inc(s_mean, 1)

            def variance(k, c):
                pe.wait_ge(s_sq, 2 * k + c + 1)
                for j in range(2):
                    for m in range(DC):
                        last = pe.matmul(ps[:, 4 * c + j, 0:GT], mean_w[:], banks(squares(c)[:, m, :])[:, j, :],
                                         start=(m == 0), stop=(m == DC - 1))
                last.then_inc(s_var, 1)

            def project(hp, par, mat, c):
                k = proj_slot(hp, mat, c)
                pairs = [(whi[par][:, mat, m, :], wlo[par][:, mat, m, :],
                          [half(xnhi, c, (m,))[:, j, :] for j in range(2)],
                          [half(xnlo, c, (m,))[:, j, :] for j in range(2)]) for m in range(DC)]
                three(pe, [ps[:, 2 * k + j, 0:GT] for j in range(2)], pairs).then_inc(s_proj, 1)

            def first_projections():
                pe.wait_ge(s_wlo, 1)
                pe.wait_ge(s_xnlo, 1)
                project(0, 0, GATE, 0)
                project(0, 0, KEY, 0)
                project(0, 0, QUERY, 0)
                pe.wait_ge(s_std, 2)
                project(0, 0, VALUE, 0)
                pe.wait_ge(s_xnlo, 2)
                for mat, read in ((GATE, s_exp), (KEY, s_ku), (QUERY, s_qraw), (VALUE, s_vt)):
                    pe.wait_ge(read, 1)
                    project(0, 0, mat, 1)

            def projections(hp, par):
                pe.wait_ge(s_wlo, hp + 1)
                pe.wait_ge(s_qraw, 2 * hp)
                pe.wait_ge(s_vt, 2 * hp)
                pe.wait_ge(s_ku, 2 * hp)
                project(hp, par, GATE, 0)
                if early(hp, 2):
                    turn_values(0, 1)
                project(hp, par, GATE, 1)
                if early(hp, 2):
                    turn_values(0, 2)
                pair_scores(hp - 1, 1 - par, 0)
                if early(hp, 2):
                    turn_values(0, 3)
                for c in range(2):
                    pe.wait_ge(s_exp, 2 * hp + 1 + c)
                    project(hp, par, KEY, c)
                for c in range(2):
                    pe.wait_ge(s_ku, 2 * hp + 1 + c)
                    project(hp, par, QUERY, c)
                for c in range(2):
                    pe.wait_ge(s_qraw, 2 * hp + 1 + c)
                    project(hp, par, VALUE, c)

            def turn_values(hp, g):
                pe.wait_ge(s_vt, 2 * hp + 1 + g // 2)
                if not (early(hp, 1) and g == 0):
                    pe.wait_ge(s_v, 4 * hp + g)
                for b in range(GB):
                    t = slice((GB * g + b) * T, (GB * g + b + 1) * T)
                    last = pe.transpose(ps[0:T, 6, b * P:(b + 1) * P], vT[:, t], ident[:])
                last.then_inc(s_vmm, 1)

            def pair_scores(a, par, g):
                pe.wait_ge(s_qa, 2 * a + 1 + g // 2)
                if not (early(a, 1) and g == 0):
                    pe.wait_ge(s_p, 4 * a + g)
                for h in range(2):
                    rows = slice(DK * h, DK * (h + 1))
                    for b in range(GB):
                        t = slice((GB * g + b) * T, (GB * g + b + 1) * T)
                        last = pe.matmul(ps[0:T, 4 + h, b * T:(b + 1) * T], kU[par][rows, t], qA[par][rows, t],
                                         start=True, stop=True)
                last.then_inc(s_pmm, 1)

            def mix(a, par, g):
                pe.wait_ge(s_p, 4 * a + g + 1)
                pe.wait_ge(s_v, 4 * a + g + 1)
                if not (early(a, 1) and g == 0):
                    pe.wait_ge(s_o, 4 * a + g)
                for b in range(GB):
                    for h in range(2):
                        last = pe.matmul(ps[DK * h:DK * (h + 1), 7, b * T:(b + 1) * T],
                                         vb[par][0:T, GB * g + b, DK * h:DK * (h + 1)],
                                         pb[g % 2][0:T, h, b * T:(b + 1) * T], start=True, stop=True)
                last.then_inc(s_omm, 1)

            def pair_step(hp, par):
                projections(hp, par)
                for g in range(G):
                    turn_values(hp, g)
                    if g + 1 < G:
                        pair_scores(hp - 1, 1 - par, g + 1)
                    mix(hp - 1, 1 - par, g)

            embed_patches(0)
            embed_patches(1)
            embed_text(0)
            embed_text(1)
            mean(0, 0)
            mean(0, 1)
            variance(0, 0)
            variance(0, 1)
            first_projections()
            pe.wait_ge(s_qraw, 2)
            turn_values(0, 0)
            pair_step(1, 1)
            with pe.Fori(2, HP, 2) as i:
                pair_step(i, 0)
                pair_step(i + 1, 1)
            pe.wait_ge(s_okcol, 1)
            pe.matmul(ps[0:1, 0, 0:1], ok_col[:, 0:1], ones[:, 0:1], start=True, stop=True).then_inc(s_okmm, 1)
            for g in range(G):
                pair_scores(HP - 1, 1, g)
                mix(HP - 1, 1, g)

            def general():
                with pe.Fori(0, HP) as hp:
                    pe.wait_ge(s_gw, 16 * hp + 16)
                    pe.wait_ge(s_gdone, hp + 1)
                    for mat in range(MATS):
                        pe.wait_ge(s_gread, 4 * hp + mat + 1)
                        for c in range(2):
                            for j in range(2):
                                for m in range(DC):
                                    w = wraw[0][:, (mat * DC + m) * P:(mat * DC + m + 1) * P]
                                    last = pe.matmul(ps[:, 2 * c + j, 0:GT], w, half(gx, c, (m,))[:, j, :],
                                                     start=(m == 0), stop=(m == DC - 1))
                        last.then_inc(s_gproj, 1)
                    with pe.Fori(0, T) as d:
                        pe.wait_ge(s_gterm, T * hp + d + 1)
                        for c in range(2):
                            for j in range(2):
                                last = pe.matmul(ps[:, 2 * c + j, 0:GT], head_sum[:], half(gprod, c)[:, j, :],
                                                 start=True, stop=True)
                        last.then_inc(s_gbc, 1)

            pe.wait_ge(s_ok, 1)
            in_range = pe.value_load(ok_sum[0:1, 0:1], min_val=0, max_val=P)
            with pe.If(in_range < P):
                general()

            def out_projection(c, m, js=(0, 1)):
                for j in js:
                    for a in range(HP):
                        last = pe.matmul(ps[:, 4 * c + 2 * m + j, 0:GT], wo[:, a, m * P:(m + 1) * P],
                                         half(oT, c, (a,))[:, j, :], start=(a == 0), stop=(a == HP - 1))
                if js[-1] == 1:
                    last.then_inc(s_womm, 1)

            pe.wait_ge(s_wo, 16)
            pe.wait_ge(s_o, 4 * HP - 2)
            pe.wait_ge(s_way, 1)
            out_projection(0, 0)
            out_projection(0, 1)
            pe.wait_ge(s_o, 4 * HP)
            pe.wait_ge(s_p, 4 * HP)
            out_projection(1, 0, (0,))
            mean(1, 0)
            out_projection(1, 0, (1,))
            variance(1, 0)
            out_projection(1, 1)

            def turn_rows(n, src, c, banks3):
                for q in range(XQ):
                    w = P if q < XQ - 1 else XTAIL
                    for m in range(DC):
                        t0 = (0 if src is xc else c * HALF) + q * P
                        cols = src[:, c, m, t0:t0 + w] if src is xc else src[:, m, t0:t0 + w]
                        o = (q % 2) * D + m * P
                        last = pe.transpose(ps[0:w, banks3[q // 2], o:o + P], cols, ident[:])
                last.then_inc(s_rows_mm, 1)

            def logits(c, bank):
                for j in range(2):
                    for m in range(DC):
                        last = pe.matmul(ps[0:E, bank + j, 0:GT], wg[:, m, :], banks(xc[:, c, m, :])[:, j, :],
                                         start=(m == 0), stop=(m == DC - 1))
                last.then_inc(s_lgmm, 1)

            def turn_logits():
                pe.wait_ge(s_lgt, 2)
                for r in range(RT):
                    t0 = min(r * P, TOK - P)
                    last = pe.transpose(ps[:, 2, r * E:(r + 1) * E], lgT[:, t0:t0 + P], ident[0:E, 0:E])
                last.then_inc(s_lgtok, 1)

            def turn_x(b, par):
                pe.wait_ge(s_gx[par], 8 * b + 16 - 8 * par)
                if not early(b, 2):
                    pe.wait_ge(s_xt, b - 1)
                for m in range(DC):
                    last = pe.transpose(ps[:, 7 * par, m * P:(m + 1) * P], xg[par][:, m * P:(m + 1) * P], ident[:])
                last.then_inc(s_tx, 1)

            def expert_of(b):
                e = b if isinstance(b, int) else b
                at = owner_i[0:1, b:b + 1] if isinstance(b, int) else owner_i[0:1, bass.ds(b, 1)]
                return pe.value_load(at, min_val=0, max_val=E - 1)

            def up(b, par):
                e = expert_of(b)
                pe.wait_ge(s_xt, b + 1)
                if not early(b, 2):
                    pe.wait_ge(s_hb, b - 1)
                for m in range(DC):
                    last = pe.matmul(ps[:, 1 + par, :], xt[par][:, m * P:(m + 1) * P],
                                     w1[:, bass.ds(e, 1), m * FH:(m + 1) * FH].rearrange("p o n -> p (o n)"),
                                     start=(m == 0), stop=(m == DC - 1))
                last.then_inc(s_up, 1)

            def turn_h(b, par):
                pe.wait_ge(s_hb, b + 1)
                if not early(b, 2):
                    pe.wait_ge(s_hr, b - 1)
                for j in range(FC):
                    last = pe.transpose(ps[:, 3 + par, j * P:(j + 1) * P], hb[par][:, j * P:(j + 1) * P], ident[:])
                last.then_inc(s_th, 1)

            def down(b, par):
                e = expert_of(b)
                pe.wait_ge(s_hr, b + 1)
                if not early(b, 2):
                    pe.wait_ge(s_yb, b - 1)
                for j in range(FC):
                    last = pe.matmul(ps[:, 5 + par, 0:D], hr[par][:, j * P:(j + 1) * P],
                                     w1[:, bass.ds(e, 1), WF + j * D:WF + (j + 1) * D].rearrange("p o n -> p (o n)"),
                                     start=(j == 0), stop=(j == FC - 1))
                last.then_inc(s_dn, 1)

            def block_step(b, par):
                up(b + 1, 1 - par)
                turn_x(b + 2, par)
                turn_h(b, par)
                down(b - 1, 1 - par)

            pe.wait_ge(s_xn, 3)
            pe.wait_ge(s_wg, 16)
            logits(0, 0)
            mean(1, 1)
            turn_rows(0, xc, 0, (2, 3, 6))
            variance(1, 1)
            pe.wait_ge(s_lgt, 1)
            turn_rows(1, hT, 0, (0, 1, 7))
            pe.wait_ge(s_rows, 1)
            turn_rows(2, hT, 1, (2, 3, 6))
            pe.wait_ge(s_xn, 4)
            logits(1, 4)
            pe.wait_ge(s_rows, 3)
            turn_logits()
            turn_rows(3, xc, 1, (0, 1, 7))
            pe.wait_ge(s_const, 7)
            pe.wait_ge(s_pick, 1)
            picks = pick[:].rearrange("p i r e -> p (i r e)")
            pe.matmul(ps[:, 4, 0:A * E], tri[:], picks, start=True, stop=True)
            pe.matmul(ps[:, 5, 0:A * E], mean_w[:], picks, start=True, stop=True).then_inc(s_count, 1)
            for a in range(A):
                if a % RT == 0:
                    pe.wait_ge(s_place, a // RT + 1)
                    pe.wait_ge(s_entry, a // RT + 1)
                last = pe.matmul(ps[:, 6, 0:3 * NB], at_place[:, a, :], entry[:, a].rearrange("p v b -> p (v b)"),
                                 start=(a == 0), stop=(a == A - 1))
            last.then_inc(s_tabmm, 1)
            pe.wait_ge(s_owner, 1)
            pe.wait_ge(s_experts, 16 * (EARLY_W + 1))
            turn_x(0, 0)
            turn_x(1, 1)
            up(0, 0)
            up(1, 1)
            turn_x(2, 0)
            turn_h(0, 0)
            block_step(1, 1)
            block_step(2, 0)
            with pe.Fori(3, NB - 3, 2) as i:
                block_step(i, 1)
                block_step(i + 1, 0)
            block_step(NB - 3, 1)
            up(NB - 1, 1)
            turn_h(NB - 2, 0)
            down(NB - 3, 1)
            turn_h(NB - 1, 1)
            down(NB - 2, 0)
            down(NB - 1, 1)

        @block.scalar
        def _(act):
            def embed_patches(c):
                act.wait_ge(s_patch_mm, c + 1)
                for m in range(DC):
                    last = act.activation(
                        hT[:, m, c * HALF:(c + 1) * HALF].rearrange("p (b t) -> p b t", t=T)[:, :, 0:NP],
                        ps[:, 4 * c + m, 0:HB * NP].rearrange("p (b t) -> p b t", t=NP),
                        ACT.Identity, bias=btok[:, m:m + 1])
                last.then_inc(s_emb, 1)

            def square(k, c):
                act.wait_ge(s_xc, 2 * k + c + 1)
                act.activation(squares(c), xc[:, c], ACT.Square).then_inc(s_sq, 1)

            def deviation(k, c):
                act.wait_ge(s_var, 2 * k + c + 1)
                act.activation(banks(std[:, c, :]), slot(2 * c), ACT.Sqrt, bias=eps[:]).then_inc(s_std, 1)

            def split_stream(k, c):
                act.wait_ge(s_xn, 2 * k + c + 1)
                act.activation(xnhi[:, :, c * HALF:(c + 1) * HALF], xc[:, c], ACT.Copy).then_inc(s_xnhi, 1)

            def load_table(func):
                act.activation(warm[:], eps[:], func)

            def split_pair(hp, par, wload):
                act.wait_ge(s_wload[par], wload)
                if not early(hp, 2):
                    act.wait_ge(s_proj, 2 * MATS * (hp - 1))
                act.activation(whi[par][:].rearrange("p a b n -> p (a b n)"), wraw[par][:, 0:WA], ACT.Copy)
                act.activation(bneg[par][:], wraw[par][:, WA:WA + 1], ACT.Copy, scale=-1.0).then_inc(s_whi, 1)

            def evacuate_gate(hp, par, c):
                tok = slice(c * HALF, (c + 1) * HALF)
                act.wait_ge(s_whi, hp + 1)
                act.wait_ge(s_proj, proj_done(hp, GATE, c))
                if not early(hp, 1):
                    act.wait_ge(s_u, 2 * hp - 1 + c)
                act.activation(half(e_g, c), slot(proj_slot(hp, GATE, c)), ACT.Exp, bias=bneg[par][:], scale=-1.0
                               ).then_inc(s_exp, 1)
                act.wait_ge(s_exp, 2 * hp + 1 + c)
                if not early(hp, 1):
                    act.wait_ge(s_scan, 2 * hp - 1 + c)
                act.activation(u_g[:, tok].rearrange("p (b t) -> p b t", t=T)[:, :, 1:T],
                               e_g[:, tok].rearrange("p (b t) -> p b t", t=T)[:, :, 1:T],
                               ACT.Copy, bias=1.0).then_inc(s_u, 1)

            def evacuate_q(hp, c):
                act.wait_ge(s_proj, proj_done(hp, QUERY, c))
                if not early(hp, 1):
                    act.wait_ge(s_qa, 2 * hp - 1 + c)
                act.activation(half(qraw, c), slot(proj_slot(hp, QUERY, c)), ACT.Copy).then_inc(s_qraw, 1)

            def evacuate_vt(hp, c):
                act.wait_ge(s_proj, proj_done(hp, VALUE, c))
                if not early(hp, 1):
                    act.wait_ge(s_vmm, 4 * hp - 2 + 2 * c)
                act.activation(half(vT, c), slot(proj_slot(hp, VALUE, c)), ACT.Copy).then_inc(s_vt, 1)

            def evacuate_v(hp, par, g):
                act.wait_ge(s_vmm, 4 * hp + g + 1)
                if not early(hp, 2) and g == 0:
                    act.wait_ge(s_omm, 4 * hp - 4)
                act.activation(vb[par][0:T, GB * g:GB * (g + 1), :].rearrange("p b n -> p (b n)"), ps[0:T, 6, :], ACT.Copy).then_inc(s_v, 1)

            def evacuate_o(a, g):
                act.wait_ge(s_omm, 4 * a + g + 1)
                act.activation(oT[:, bass.ds(a, 1), g * GT:(g + 1) * GT], ps[:, 7:8, 0:GT], ACT.Copy).then_inc(s_o, 1)

            def pair_step(hp, par, wload, tail=False):
                evacuate_gate(hp, par, 0)
                if early(hp, 2):
                    evacuate_v(0, 0, 1)
                evacuate_gate(hp, par, 1)
                if early(hp, 2):
                    evacuate_v(0, 0, 2)
                    evacuate_v(0, 0, 3)
                if not tail:
                    split_pair(hp + 1, 1 - par, wload)
                evacuate_q(hp, 0)
                evacuate_q(hp, 1)
                evacuate_vt(hp, 0)
                evacuate_vt(hp, 1)
                for g in range(G):
                    evacuate_v(hp, par, g)
                    evacuate_o(hp - 1, g)

            act.wait_ge(s_const, 4)
            load_table(ACT.Sqrt)
            act.wait_ge(s_wr, 32)
            embed_patches(0)
            embed_patches(1)
            split_pair(0, 0, 16)
            square(0, 0)
            square(0, 1)
            deviation(0, 0)
            deviation(0, 1)
            load_table(ACT.Exp)
            split_stream(0, 0)
            evacuate_gate(0, 0, 0)
            split_stream(0, 1)
            evacuate_q(0, 0)
            evacuate_vt(0, 0)
            evacuate_gate(0, 0, 1)
            split_pair(1, 1, 16)
            evacuate_q(0, 1)
            evacuate_vt(0, 1)
            evacuate_v(0, 0, 0)
            pair_step(1, 1, 32)
            with act.Fori(2, HP - 2, 2) as i:
                pair_step(i, 0, 8 * i + 16)
                pair_step(i + 1, 1, 8 * i + 32)
            pair_step(HP - 2, 0, 16 * (HP // 2))
            pair_step(HP - 1, 1, 0, tail=True)
            for g in range(G):
                evacuate_o(HP - 1, g)

            def general():
                with act.Fori(0, HP) as hp:
                    act.wait_ge(s_gw, 16 * hp + 16)
                    act.wait_ge(s_gdone, hp + 1)
                    act.activation(bneg[0][:], wraw[0][:, WA:WA + 1], ACT.Copy, scale=-1.0).then_inc(s_gset, 1)
                    act.wait_ge(s_gset, hp + 1)
                    act.wait_ge(s_gproj, 4 * hp + 1)
                    for c in range(2):
                        last = act.activation(half(ga, c), slot(c), ACT.Exp, bias=bneg[0][:], scale=-1.0)
                    last.then_inc(s_gread, 1)

            act.wait_ge(s_ok, 1)
            in_range = act.value_load(ok_sum[0:1, 0:1], min_val=0, max_val=P)
            with act.If(in_range < P):
                general()

            def rows(n, t, c, banks3, tail):
                act.wait_ge(s_rows_mm, n + 1)
                act.activation(t[:, c, 0:4].rearrange("p (a q) d -> p a (q d)", a=2),
                               ps[:, banks3:banks3 + 2, :], ACT.Copy)
                act.activation(t[0:XTAIL, c, 4], ps[0:XTAIL, tail, 0:D], ACT.Copy).then_inc(s_rows, 1)

            def relu(b, par):
                act.wait_ge(s_th, b + 1)
                if not early(b, 2):
                    act.wait_ge(s_dn, b - 1)
                act.activation(hr[par][:], ps[:, 3 + par, :], ACT.Relu).then_inc(s_hr, 1)

            def scale(b, par):
                act.wait_ge(s_yb, b + 1)
                if not early(b, 2):
                    act.wait_ge(s_added, 16 * b - 16)
                col = shares[:, b:b + 1] if isinstance(b, int) else shares[:, bass.ds(b, 1)]
                act.activation(ys[par][:], yb[par][:], ACT.Copy, scale=col).then_inc(s_ys, 1)

            load_table(ACT.Sqrt)
            square(1, 0)
            deviation(1, 0)
            act.wait_ge(s_lgmm, 1)
            act.activation(half(lgT, 0), ps[0:E, 0:2, 0:GT], ACT.Copy).then_inc(s_lgt, 1)
            square(1, 1)
            rows(0, xrow, 0, 2, 6)
            deviation(1, 1)
            load_table(ACT.Exp)
            rows(1, hrow, 0, 0, 7)
            rows(2, hrow, 1, 2, 6)
            act.wait_ge(s_lgmm, 2)
            act.activation(half(lgT, 1), ps[0:E, 4:6, 0:GT], ACT.Copy).then_inc(s_lgt, 1)
            act.wait_ge(s_prob, 1)
            act.activation(pr[:], lg[:], ACT.Exp).then_inc(s_exps, 1)
            rows(3, xrow, 1, 0, 7)
            act.wait_ge(s_share, 1)
            act.activation(share_hi[:], share[:], ACT.Copy).then_inc(s_share, 1)
            act.wait_ge(s_tab, 3)
            relu(0, 0)
            relu(1, 1)
            scale(0, 0)
            relu(2, 0)
            scale(1, 1)
            with act.Fori(3, NB - 1, 2) as i:
                relu(i, 1)
                scale(i - 1, 0)
                relu(i + 1, 0)
                scale(i, 1)
            relu(NB - 1, 1)
            scale(NB - 2, 0)
            scale(NB - 1, 1)

        @block.vector
        def _(dve):
            links = [0]

            def link(ins):
                links[0] += 1
                ins.then_inc(s_link, 1)
                dve.wait_ge(s_link, links[0])

            dve.wait_ge(s_idx_in, 16)
            link(dve.tensor_copy(idx_f[:], idx_i[:]))
            link(dve.tensor_scalar(idx_n[:], idx_f[:], 0.0, float(VOCAB), ALU.is_lt, ALU.mult))
            link(dve.tensor_tensor(idx_f[:], idx_f[:], idx_n[:], ALU.add))
            dve.tensor_scalar(idx_u[:], idx_f[:], 0.0, float(VOCAB - 1), ALU.max, ALU.min).then_inc(s_idx, 1)
            dve.memset(u_ok[:], 1.0).then_inc(s_uok, 1)
            dve.wait_ge(s_gt_mm, 1)
            dve.tensor_copy(gT[:], ps[:, 7, :]).then_inc(s_gt, 1)

            def embed_text(c):
                dve.wait_ge(s_text_mm, c + 1)
                for m in range(DC):
                    last = dve.tensor_copy(
                        hT[:, m, c * HALF:(c + 1) * HALF].rearrange("p (b t) -> p b t", t=T)[:, :, NP:T],
                        ps[:, 4 * c + 2 + m, 0:HB * NT].rearrange("p (b t) -> p b t", t=NT))
                last.then_inc(s_txt, 1)

            def centre(k, c):
                dve.wait_ge(s_mean, 2 * k + c + 1)
                if k == 0:
                    dve.wait_ge(s_emb, c + 1)
                    dve.wait_ge(s_txt, c + 1)
                else:
                    dve.wait_ge(s_h2, 2 * (c + 1))
                for m in range(DC):
                    last = dve.tensor_tensor(banks(xc[:, c, m, :]), half(hT, c, (m,)), slot(2 * c), ALU.subtract)
                last.then_inc(s_xc, 1)

            def normalise(k, c):
                n = 2 * k + c
                dve.wait_ge(s_std, n + 1)
                dve.reciprocal(rstd(c), std[:, c, :]).then_inc(s_rstd, 1)
                dve.wait_ge(s_rstd, n + 1)
                dve.wait_ge(s_sq, n + 1)
                for m in range(DC):
                    last = dve.tensor_tensor(xc[:, c, m, :], xc[:, c, m, :], rstd(c), ALU.mult)
                last.then_inc(s_xn, 1)

            def split_stream(k, c):
                dve.wait_ge(s_xnhi, 2 * k + c + 1)
                tok = slice(c * HALF, (c + 1) * HALF)
                dve.tensor_tensor(xnlo[:, :, tok], xc[:, c], xnhi[:, :, tok].bitcast(F32), ALU.subtract
                                  ).then_inc(s_xnlo, 1)

            def decay(hp, par):
                for c in range(2):
                    dve.wait_ge(s_u, 2 * hp + c + 1)
                    if not early(hp, 1):
                        dve.wait_ge(s_a, 4 * hp - 2 + 2 * c)
                    dve.tensor_tensor_scan(U[:, c * HALF:(c + 1) * HALF], u_g[:, c * HALF:(c + 1) * HALF], first[:],
                                           1.0, ALU.mult, ALU.add).then_inc(s_scan, 1)
                    dve.wait_ge(s_scan, 2 * hp + c + 1)
                    dve.wait_ge(s_proj, proj_done(hp, KEY, c))
                    if c == 0 and not early(hp, 2):
                        dve.wait_ge(s_pmm, 4 * hp - 4)
                    dve.tensor_tensor(half(kU[par], c), slot(proj_slot(hp, KEY, c)), half(U, c), ALU.mult).then_inc(s_ku, 1)
                dve.wait_ge(s_uok, hp + 1)
                dve.scalar_tensor_tensor(u_ok[:], U[:].rearrange("p (b t) -> p b t", t=T)[:, :, T - 1], U_LIMIT,
                                         u_ok[:], ALU.is_le, ALU.mult).then_inc(s_uok, 1)

            def invert(hp, g):
                if not early(hp, 1):
                    dve.wait_ge(s_qa, 2 * hp - 1 + g // 2)
                dve.reciprocal(invU[:, g * GT:(g + 1) * GT], U[:, g * GT:(g + 1) * GT]).then_inc(s_a, 1)

            def mask(a, g):
                dve.wait_ge(s_pmm, 4 * a + g + 1)
                if not (early(a, 1) and g < 2):
                    dve.wait_ge(s_omm, 4 * a + g - 1)
                dve.tensor_tensor(pb[g % 2][0:T].bitcast(U32), ps[0:T, 4:6, 0:GT].bitcast(U32), causal_bits[0:T],
                                  ALU.bitwise_and).then_inc(s_p, 1)

            def pair_step(hp, par):
                decay(hp, par)
                mask(hp - 1, 0)
                for g in range(3):
                    invert(hp, g)
                mask(hp - 1, 1)
                invert(hp, 3)
                mask(hp - 1, 2)
                mask(hp - 1, 3)

            embed_text(0)
            embed_text(1)
            centre(0, 0)
            centre(0, 1)
            normalise(0, 0)
            split_stream(0, 0)
            normalise(0, 1)
            split_stream(0, 1)
            dve.wait_ge(s_const, 6)
            dve.tensor_scalar(causal_bits[:].bitcast(I32), causal[:], -1.0, None, ALU.mult)
            dve.wait_ge(s_first, 1)
            decay(0, 0)
            for g in range(G):
                invert(0, g)
            pair_step(1, 1)
            with dve.Fori(2, HP, 2) as i:
                pair_step(i, 0)
                pair_step(i + 1, 1)
            dve.wait_ge(s_uok, HP + 1)
            dve.tensor_reduce(ok_col[:], u_ok[:], AX_X, ALU.min).then_inc(s_okcol, 1)
            dve.wait_ge(s_okmm, 1)
            dve.tensor_copy(ok_sum[:], ps[0:1, 0, 0:1]).then_inc(s_ok, 1)
            for g in range(G):
                mask(HP - 1, g)
            dve.wait_ge(s_ok, 1)

            def general():
                dve.wait_ge(s_o, 4 * HP)
                dve.wait_ge(s_qa, 2 * HP)
                dve.tensor_tensor(gx[:], xnhi[:].bitcast(F32), xnlo[:].bitcast(F32), ALU.add)
                dve.memset(head_sum[:], 0.0)
                dve.drain()
                dve.memset(head_sum[0:DK, 0:DK], 1.0)
                dve.memset(head_sum[DK:P, DK:P], 1.0).then_inc(s_gread, 1)
                dve.drain().then_inc(s_gdone, 1)

                def by_batch(t):
                    return t[:].rearrange("p (b t) -> p b t", t=T)

                with dve.Fori(0, HP) as hp:
                    for i, dst in ((KEY, gk[0]), (QUERY, gq), (VALUE, gv[0])):
                        dve.wait_ge(s_gproj, 4 * hp + i + 1)
                        for c in range(2):
                            last = dve.tensor_copy(half(dst, c), slot(c))
                        last.then_inc(s_gread, 1)
                    dve.tensor_scalar(ga[:], ga[:], 1.0, None, ALU.add)
                    dve.drain()
                    dve.reciprocal(ga[:], ga[:])
                    dve.memset(gsum[:], 0.0)
                    dve.drain()
                    with dve.Fori(0, T, 2) as d:
                        for i in range(2):
                            dve.tensor_tensor(gprod[:], gq[:], gk[i][:], ALU.mult).then_inc(s_gterm, 1)
                            dve.tensor_tensor(by_batch(gk[1 - i])[:, :, 1:T], by_batch(ga)[:, :, 1:T],
                                              by_batch(gk[i])[:, :, 0:T - 1], ALU.mult)
                            dve.memset(by_batch(gk[1 - i])[:, :, 0:1], 0.0)
                            dve.tensor_copy(by_batch(gv[1 - i])[:, :, 1:T], by_batch(gv[i])[:, :, 0:T - 1])
                            dve.memset(by_batch(gv[1 - i])[:, :, 0:1], 0.0)
                            dve.wait_ge(s_gbc, T * hp + d + i + 1)
                            for c in range(2):
                                dve.tensor_tensor(half(gprod, c), slot(c), half(gv[i], c), ALU.mult)
                            dve.drain()
                            dve.tensor_tensor(gsum[:], gsum[:], gprod[:], ALU.add)
                            dve.drain()
                    dve.tensor_copy(oT[:, bass.ds(hp, 1), :], gsum[:].unsqueeze(1))
                    dve.drain().then_inc(s_gdone, 1)

            in_range = dve.value_load(ok_sum[0:1, 0:1], min_val=0, max_val=P)
            with dve.If(in_range < P):
                general()
            dve.drain().then_inc(s_way, 1)

            def residual(c, m):
                dve.wait_ge(s_womm, 2 * c + m + 1)
                dve.tensor_tensor(half(hT, c, (m,)), half(hT, c, (m,)), slot(2 * c + m), ALU.add).then_inc(s_h2, 1)

            residual(0, 0)
            residual(0, 1)
            centre(1, 0)
            residual(1, 0)
            normalise(1, 0)
            residual(1, 1)
            centre(1, 1)

            normalise(1, 1)

            def wide(t):
                return t.unsqueeze(2).to_broadcast([P, RT, E])

            logits = ps[:, 2, 0:RT * E].rearrange("p (r e) -> p r e", e=E)
            dve.wait_ge(s_const, 7)
            dve.wait_ge(s_lgtok, 1)
            link(dve.tensor_reduce(rs[:, 0, :], logits, AX_X, ALU.max))
            dve.tensor_tensor(lg[:], logits, wide(rs[:, 0, :]), ALU.subtract).then_inc(s_prob, 1)
            dve.wait_ge(s_exps, 1)
            link(dve.tensor_reduce(rs[:, 1, :], pr[:], AX_X, ALU.add))
            link(dve.reciprocal(rs[:, 1, :], rs[:, 1, :]))
            link(dve.tensor_tensor(pr[:], pr[:], wide(rs[:, 1, :]), ALU.mult))
            for r in range(RT):
                last = dve.max(top[:, r, :], pr[:, r, :])
            link(last)
            for r in range(RT):
                last = dve.max_index(topi[:, r, :], top[:, r, :], pr[:, r, :])
            link(last)
            link(dve.tensor_copy(topf[:], topi[:]))

            def by_pick(t):
                return t[:, :, 0:PICKS].rearrange("p r i -> p i r")

            link(dve.tensor_tensor(pick[:], expert_no[:],
                                   by_pick(topf).unsqueeze(3).to_broadcast([P, PICKS, RT, E]), ALU.is_equal))
            dve.memset(pick[0:DUP, :, RT - 1, :], 0.0).then_inc(s_pick, 1)
            link(dve.tensor_tensor(rs[:, 2, :], top[:, :, 0], top[:, :, 1], ALU.add))
            link(dve.reciprocal(rs[:, 2, :], rs[:, 2, :]))
            link(dve.tensor_tensor(share[:], by_pick(top),
                                   rs[:, 2, :].unsqueeze(1).to_broadcast([P, PICKS, RT]), ALU.mult))
            dve.memset(share[0:DUP, :, RT - 1], 0.0).then_inc(s_share, 1)
            dve.wait_ge(s_share, 2)
            dve.tensor_tensor(share_lo[:], share[:], share_hi[:].bitcast(F32), ALU.subtract).then_inc(s_share, 1)

            flat = "p e a -> p (e a)"
            dve.wait_ge(s_count, 1)
            link(dve.tensor_scalar(total[:], ps[:, 5, 0:A * E].rearrange("p (a e) -> p e a", e=E), float(D), None,
                                   ALU.mult))
            link(dve.tensor_tensor_scan(upto[:].rearrange(flat), seg[:].rearrange(flat), total[:].rearrange(flat),
                                        0.0, ALU.mult, ALU.add))
            link(dve.tensor_tensor(more[:], upto[:, :, A - 1:A].to_broadcast([P, E, BN - 1]), steps[:], ALU.is_gt))
            link(dve.tensor_reduce(blocks[:, 0, :], more[:], AX_X, ALU.add))
            link(dve.tensor_scalar(blocks[:, 0, :], blocks[:, 0, :], 1.0, None, ALU.add))
            link(dve.tensor_tensor_scan(blocks[:, 1, :], ones_e[:], blocks[:, 0, :], 0.0, ALU.mult, ALU.add))
            link(dve.tensor_tensor(blocks[:, 1, :], blocks[:, 1, :], blocks[:, 0, :], ALU.subtract))
            link(dve.tensor_scalar(blocks[:, 2, :], blocks[:, 1, :], float(P), None, ALU.mult))
            link(dve.tensor_tensor(upto[:], upto[:], total[:], ALU.subtract))
            link(dve.tensor_tensor(upto[:], upto[:], blocks[:, 2, :].unsqueeze(2).to_broadcast([P, E, A]), ALU.add))
            link(dve.tensor_tensor(pos_e[:], ps[:, 4, 0:A * E].rearrange("p (a e) -> p a e", e=E),
                                   upto[:].rearrange("p e a -> p a e"), ALU.add))
            link(dve.tensor_tensor(pos_e[:], pos_e[:], pick[:].rearrange("p i r e -> p (i r) e"), ALU.mult))
            link(dve.tensor_reduce(pos[:], pos_e[:], AX_X, ALU.add))
            link(dve.tensor_copy(pos_i[:], pos[:]))
            link(dve.tensor_scalar(pos_i[:], pos_i[:], P - 1, None, ALU.bitwise_and))
            link(dve.tensor_copy(place_of[:], pos_i[:]))
            link(dve.tensor_tensor(border[:], pos[:], place_of[:], ALU.subtract))
            dve.tensor_tensor(in_block[:], block_start[:].unsqueeze(1).to_broadcast([P, A, NB]),
                              border[:].unsqueeze(2).to_broadcast([P, A, NB]), ALU.is_equal).then_inc(s_off, 1)
            for i in range(PICKS):
                a = slice(i * RT, (i + 1) * RT)
                dve.tensor_tensor(at_place[:, a], place[:].unsqueeze(1).to_broadcast([P, RT, P]),
                                  place_of[:, a].unsqueeze(2).to_broadcast([P, RT, P]), ALU.is_equal
                                  ).then_inc(s_place, 1)
            link(dve.tensor_tensor(passed[:], blocks[:, 1, :].unsqueeze(1).to_broadcast([P, NB, E]), block_no[:],
                                   ALU.is_le))
            link(dve.tensor_reduce(owner[:], passed[:], AX_X, ALU.add))
            dve.tensor_scalar(owner_i[:], owner[:], -1.0, None, ALU.add).then_inc(s_owner, 1)
            dve.wait_ge(s_tabmm, 1)
            link(dve.tensor_copy(table[:], ps[:, 6, 0:3 * NB].rearrange("p (v b) -> p v b", b=NB)))
            dve.tensor_scalar(gather_u[:], table[:, 0, :], -1.0, 0.0, ALU.add, ALU.max).then_inc(s_tab, 1)
            link(dve.tensor_scalar(tab[:, 0, :], table[:, 0, :], 0.5, None, ALU.is_lt))
            link(dve.tensor_scalar(tab[:, 0, :], tab[:, 0, :], spare_no[:], -1.0, ALU.mult, ALU.add))
            dve.tensor_tensor(scatter_u[:], table[:, 0, :], tab[:, 0, :], ALU.add).then_inc(s_tab, 1)
            dve.tensor_tensor(shares[:], table[:, 1, :], table[:, 2, :], ALU.add).then_inc(s_tab, 1)

            def copy_x(b, par):
                dve.wait_ge(s_tx, b + 1)
                if not early(b, 2):
                    dve.wait_ge(s_up, b - 1)
                dve.tensor_copy(xt[par][:], ps[:, 7 * par, 0:D]).then_inc(s_xt, 1)

            def owner_of(b):
                at = owner_i[0:1, b:b + 1] if isinstance(b, int) else owner_i[0:1, bass.ds(b, 1)]
                return dve.value_load(at, min_val=0, max_val=E - 1)

            def add_b1(b, par):
                e = owner_of(b)
                dve.wait_ge(s_up, b + 1)
                if not early(b, 2):
                    dve.wait_ge(s_th, b - 1)
                dve.tensor_tensor(hb[par][:], ps[:, 1 + par, :],
                                  bias[:, bass.ds(e, 1), 0:FH].rearrange("p o n -> p (o n)"), ALU.add
                                  ).then_inc(s_hb, 1)

            def add_b2(b, par):
                e = owner_of(b)
                dve.wait_ge(s_dn, b + 1)
                if not early(b, 2):
                    dve.wait_ge(s_ys, b - 1)
                dve.tensor_tensor(yb[par][:], ps[:, 5 + par, 0:D],
                                  bias[:, bass.ds(e, 1), FH:FH + D].rearrange("p o n -> p (o n)"), ALU.add
                                  ).then_inc(s_yb, 1)

            def block_step(b, par):
                add_b1(b + 1, 1 - par)
                copy_x(b + 2, par)
                add_b2(b - 1, 1 - par)

            dve.wait_ge(s_owner, 1)
            dve.wait_ge(s_bias, 16)
            copy_x(0, 0)
            copy_x(1, 1)
            add_b1(0, 0)
            add_b1(1, 1)
            copy_x(2, 0)
            block_step(1, 1)
            block_step(2, 0)
            with dve.Fori(3, NB - 3, 2) as i:
                block_step(i, 1)
                block_step(i + 1, 0)
            block_step(NB - 3, 1)
            add_b1(NB - 1, 1)
            add_b2(NB - 3, 1)
            add_b2(NB - 2, 0)
            add_b2(NB - 1, 1)

        @block.gpsimd
        def _(pool):
            pool.memset(ident[:], 0.0).then_inc(s_const, 1)
            pool.memset(mean_w[:], 1.0 / D).then_inc(s_const, 1)
            pool.memset(eps[:], LN_EPS).then_inc(s_const, 1)
            pool.memset(ones[:], 1.0).then_inc(s_const, 1)
            pool.wait_ge(s_const, 4)
            pool.affine_select(out=ident[:], in_=ident[:], compare_op=ALU.not_equal, fill=1.0, base=0,
                               pattern=[[-1, P]], channel_multiplier=1).then_inc(s_const, 1)
            pool.wait_ge(s_idx, 1)
            for g in range(G):
                pool.indirect_dma_start(out=gath[:, g, :], out_offset=None, in_=w_l,
                                        in_offset=bass.IndirectOffsetOnAxis(ap=idx_u[:, g:g + 1], axis=0),
                                        bounds_check=VOCAB - 1).then_inc(s_gath, 16)
            pool.memset(first[:], 0.0)
            pool.memset(causal[:], 1.0).then_inc(s_link2, 1)
            pool.wait_ge(s_link2, 1)
            pool.memset(first[:].rearrange("p (b t) -> p b t", t=T)[:, :, 0:1], 1.0)
            keep = causal[:].rearrange("p h (b t) -> p (h b) t", t=T)
            pool.affine_select(out=keep, in_=keep, compare_op=ALU.is_ge, fill=0.0, base=0,
                               pattern=[[0, 2 * GB], [1, T]], channel_multiplier=-1).then_inc(s_const, 1)

            def split_pair(hp, par):
                pool.wait_ge(s_whi, hp + 1)
                pool.tensor_tensor(wlo[par][:].rearrange("p a b n -> p (a b n)"), wraw[par][:, 0:WA],
                                   whi[par][:].bitcast(F32).rearrange("p a b n -> p (a b n)"), ALU.subtract
                                   ).then_inc(s_wlo, 1)

            def scale_q(hp, par):
                for c in range(2):
                    pool.wait_ge(s_qraw, 2 * hp + 1 + c)
                    pool.wait_ge(s_a, 4 * hp + 2 + 2 * c)
                    if c == 0 and not early(hp, 2):
                        pool.wait_ge(s_pmm, 4 * hp - 4)
                    tok = slice(c * HALF, (c + 1) * HALF)
                    pool.tensor_tensor(qA[par][:, tok], qraw[:, tok], invU[:, tok], ALU.mult).then_inc(s_qa, 1)

            def pair_step(hp, par, tail=False):
                if not tail:
                    split_pair(hp + 1, 1 - par)
                scale_q(hp, par)

            split_pair(0, 0)
            pool.memset(u_g[:].rearrange("p (b t) -> p b t", t=T)[:, :, 0:1], 0.0).then_inc(s_first, 1)
            split_pair(1, 1)
            scale_q(0, 0)
            pair_step(1, 1)
            with pool.Fori(2, HP - 2, 2) as i:
                pair_step(i, 0)
                pair_step(i + 1, 1)
            pair_step(HP - 2, 0)
            pair_step(HP - 1, 1, tail=True)

            def iota(t, pattern, base, step=0):
                return pool.iota(t, pattern=pattern, base=base, channel_multiplier=step,
                                 allow_small_or_imprecise_dtypes=True)

            iota(expert_no[:], [[0, PICKS], [0, RT], [1, E]], 0)
            iota(steps[:], [[0, E], [P, BN - 1]], P)
            iota(block_start[:], [[P, NB]], 0)
            iota(block_no[:], [[1, NB], [0, E]], 0)
            iota(place[:], [[1, P]], 0)
            iota(row_no[:, :, 0:RT - 1], [[0, PICKS], [P, RT - 1]], 1, 1)
            iota(row_no[:, :, RT - 1:RT], [[0, PICKS], [0, 1]], TOK - P + 1, 1)
            iota(spare_no[:], [[0, 1]], TOK + 1, 1)
            pool.memset(ones_e[:], 1.0)
            pool.memset(seg[:], 1.0)
            pool.memset(tri[:], 1.0).then_inc(s_link2, 1)
            pool.wait_ge(s_link2, 2)
            pool.memset(seg[:, :, 0:1], 0.0)
            pool.memset(row_no[0:DUP, :, RT - 1:RT], 0.0)
            pool.affine_select(out=tri[:], in_=tri[:], compare_op=ALU.is_gt, fill=0.0, base=0,
                               pattern=[[1, P]], channel_multiplier=-1).then_inc(s_const, 1)
            pool.wait_ge(s_off, 1)
            pool.wait_ge(s_share, 3)
            pool.wait_ge(s_const, 7)

            for i in range(PICKS):
                a = slice(i * RT, (i + 1) * RT)
                for v, t in enumerate((row_no, share_hi, share_lo)):
                    t = t[:, i] if v == 0 else t[:, i].bitcast(F32)
                    last = pool.tensor_tensor(entry[:, a, v, :], in_block[:, a],
                                              t.unsqueeze(2).to_broadcast([P, RT, NB]), ALU.mult)
                last.then_inc(s_entry, 1)

            def gather(b):
                par = b % 2
                if b >= 2:
                    pool.wait_ge(s_tx, b - 1)
                pool.indirect_dma_start(out=xg[par][:], out_offset=None, in_=xrows,
                                        in_offset=bass.IndirectOffsetOnAxis(ap=gather_u[:, b:b + 1], axis=0),
                                        bounds_check=TOK - 1).then_inc(s_gx[par], 16)

            def scatter(b):
                if b >= 1:
                    pool.wait_ge(s_added, 16 * b)
                pool.wait_ge(s_ys, b + 1)
                pool.indirect_dma_start(out=out,
                                        out_offset=bass.IndirectOffsetOnAxis(ap=scatter_u[:, b:b + 1], axis=0),
                                        in_=ys[b % 2][:], in_offset=None, bounds_check=TOK + P - 1,
                                        compute_op=ALU.add).then_inc(s_added, 16)

            pool.wait_ge(s_tab, 1)
            pool.wait_ge(s_xrows, 64)
            for b in range(4):
                gather(b)
            pool.wait_ge(s_tab, 2)
            pool.wait_ge(s_hrows, 80)
            for b in range(NB):
                if b + 4 < NB:
                    gather(b + 4)
                scatter(b)


def kernel(x, x_txt, L0_tok_W, L0_tok_b, L0_txt_weight_l, L0_txt_weight_r, L0_attn_W_q, L0_attn_W_k, L0_attn_W_v,
           L0_attn_W_gate, L0_attn_b_gate, L0_attn_W_o, L0_ffn_Wg, L0_ffn_W1, L0_ffn_b1, L0_ffn_W2, L0_ffn_b2):
    import concourse.bacc as bacc
    from concourse.bass_utils import run_bass_kernel_spmd as run

    a = np.asarray
    c = np.ascontiguousarray
    runs = a(x).transpose(0, 2, 1, 3).reshape(2, HB * NP, PC, P)

    def rows(w, n):
        w = a(w)
        return w.reshape(n, P, w.shape[-1]).transpose(1, 0, 2)

    mats = [a(w).reshape(DC, P, HP, P).transpose(2, 1, 0, 3).reshape(HP, P, DC * P)
            for w in (L0_attn_W_gate, L0_attn_W_k, L0_attn_W_q, L0_attn_W_v)]
    arrays = {
        "x_idx": c(a(x_txt).reshape(G, P).T),
        "patches": c(runs.transpose(0, 3, 2, 1)),
        "w_tok": c(rows(a(L0_tok_W).T, PC)),
        "b_tok": c(a(L0_tok_b).reshape(DC, P).T),
        "w_l": c(a(L0_txt_weight_l)),
        "w_r": c(a(L0_txt_weight_r)),
        "w_attn": np.concatenate([*mats, a(L0_attn_b_gate).reshape(HP, P, 1)], axis=2),
        "w_o": c(rows(L0_attn_W_o, HP)),
        "w_gate": c(rows(L0_ffn_Wg, DC)),
        "w_ffn": np.concatenate([
            a(L0_ffn_W1).reshape(E, DC, P, FH).transpose(0, 2, 1, 3).reshape(E, P, WF),
            a(L0_ffn_W2).reshape(E, FC, P, D).transpose(0, 2, 1, 3).reshape(E, P, WF)], axis=2),
        "b_ffn": np.concatenate([a(L0_ffn_b1), a(L0_ffn_b2)], axis=1).reshape(1, E * (FH + D)),
    }
    nc = bacc.Bacc("TRN2", target_bir_lowering=False, num_devices=1)
    ins = {n: nc.dram_tensor(n, v.shape, mybir.dt.from_np(v.dtype), kind="ExternalInput").ap()
           for n, v in arrays.items()}
    out = nc.dram_tensor("out", (TOK + P, D), F32, kind="ExternalOutput").ap()
    xrows = nc.dram_tensor("xrows", (TOK, D), F32, kind="Internal").ap()
    build(nc, **ins, out=out, xrows=xrows)
    got = run(nc, [arrays], core_ids=[0]).results[0]["out"]
    return got[:TOK].reshape(B, T, D)
```

```python
from contextlib import ExitStack

import numpy as np

import concourse.bass as bass
from concourse import mybir

F32 = mybir.dt.float32
F32R = mybir.dt.float32r
I32 = mybir.dt.int32
U32 = mybir.dt.uint32
ALU = mybir.AluOpType
ACT = mybir.ActivationFunctionType
AX_X = mybir.AxisListType.X

P = 128
B, NP, NT = 16, 36, 32
T = NP + NT
TOK = B * T
D, PD = 256, 768
KE = 128
VOCAB = 32000
H, DK = 16, 64
HP = H // 2
E, FH = 8, 512
DC, PC, FC = D // P, PD // P, FH // P
HALF = TOK // 2
GB = 4
G = B // GB
GT = GB * T
HB = B // 2
U_LIMIT = 1e25
LN_EPS = 1e-5
MATS = 4
GATE, KEY, QUERY, VALUE = range(MATS)
WA = MATS * DC * P
WF = DC * FH
EP = 3
RT = -(-TOK // P)
DUP = RT * P - TOK
PICKS = 2
A = PICKS * RT
NB = (PICKS * TOK - E) // P + E
BN = -(-TOK // P)
XQ = -(-HALF // P)
XTAIL = HALF - (XQ - 1) * P
XG = 3
UNROLL = 2 * XG
assert (NB - 6) % UNROLL == 0
EARLY_W = 6


def build(nc, x_idx, patches, w_tok, b_tok, w_l, w_r, w_attn, w_o, w_gate, w_1, w_2, b_1, b_2, out, xrows):
    with ExitStack() as ctx:
        def sem(name):
            return ctx.enter_context(nc.semaphore(name))

        cursor = [16512]

        def sb(name, shape, dt=F32, at=None):
            c = cursor if at is None else at
            t = nc.alloc_sbuf_tensor_at(name, shape, dt, offset=c[0])
            c[0] += -(-int(np.prod(shape[1:])) * 4 // 32) * 32
            assert c[0] <= nc.sbuf_usable_end
            return t

        hT = sb("hT", [P, DC, TOK])
        at_xn = cursor[0]
        xnhi = sb("xnhi", [P, DC, TOK], F32R)
        xnlo = sb("xnlo", [P, DC, TOK], F32R)
        start_o = cursor[0]
        oT = sb("oT", [P, HP, TOK])
        wo = sb("wo", [P, HP, D])
        end_o = cursor[0]
        causal = sb("causal", [P, 2, GT])
        causal_bits = sb("causal_bits", [P, 2, GT], U32)
        first = sb("first", [P, HALF])
        ident = sb("ident", [P, P])
        mean_w = sb("mean_w", [P, P])
        ones = sb("ones", [P, 1])
        eps = sb("eps", [P, 1])
        warm = sb("warm", [P, 1])
        btok = sb("btok", [P, DC])
        u_ok = sb("u_ok", [P, B])
        ok_col = sb("ok_col", [P, 1])
        ok_sum = sb("ok_sum", [1, 1], I32)
        b1 = sb("b1", [P, E, FC])
        wg = sb("wg", [P, DC, E])
        tri = sb("tri", [P, P])
        expert_no = sb("expert_no", [P, PICKS, RT, E])
        seg = sb("seg", [P, E, A])
        steps = sb("steps", [P, E, BN])
        block_start = sb("block_start", [P, NB])
        block_no = sb("block_no", [P, NB, E])
        place = sb("place", [P, P])
        row_no = sb("row_no", [P, PICKS, RT])
        ones_e = sb("ones_e", [P, E])
        spare_no = sb("spare_no", [P, 1])
        lgT = sb("lgT", [E, TOK])
        lg = sb("lg", [P, RT, E])
        pr = sb("pr", [P, RT, E])
        top = sb("top", [P, RT, 8])
        topi = sb("topi", [P, RT, 8], U32)
        topf = sb("topf", [P, RT, 8])
        rs = sb("rs", [P, 3, RT])
        idx_i = sb("idx_i", [P, G], I32)
        idx_f = sb("idx_f", [P, G])
        idx_n = sb("idx_n", [P, G])
        idx_u = sb("idx_u", [P, G], U32)

        start_w = cursor[0]
        pt = sb("pt", [P, 2, PC, HB * NP])
        wtok = sb("wtok", [P, PC, D])
        gath = sb("gath", [P, G, KE])
        gT = sb("gT", [P, B * NT])
        wr = sb("wr", [P, D])

        start = cursor[0]
        e_g = sb("e_g", [P, TOK])
        u_g = sb("u_g", [P, TOK])
        U = sb("U", [P, TOK])
        invU = sb("invU", [P, TOK])
        qraw = sb("qraw", [P, TOK])
        kU = [sb(f"kU{i}", [P, TOK]) for i in range(2)]
        ln_end = cursor[0]
        qA = [sb(f"qA{i}", [P, TOK]) for i in range(2)]
        vb = [sb(f"vb{i}", [P, B, P]) for i in range(2)]
        pb = [sb(f"pb{i}", [P, 2, GT]) for i in range(2)]
        pb_end = cursor[0]
        wraw = [sb(f"wraw{i}", [P, WA + 1]) for i in range(2)]
        bneg = [sb(f"bneg{i}", [P, 1]) for i in range(2)]
        whi = [sb(f"whi{i}", [P, MATS, DC, P], F32R) for i in range(2)]
        wlo = [sb(f"wlo{i}", [P, MATS, DC, P], F32R) for i in range(2)]
        attn_end = cursor[0]
        over = [start_w]
        w1 = sb("w1", [P, E, WF], at=over)
        w1lo = nc.alloc_sbuf_tensor_at("w1lo", [P, E, WF], F32R, offset=start_w)
        assert EARLY_W * WF * 4 <= start - start_w
        w2 = sb("w2", [P, E, WF], at=over)
        w1hi = sb("w1hi", [P, E, WF], F32R, at=over)
        b2 = sb("b2", [P, E, D], at=over)
        hrow = sb("hrow", [P, 2, XQ, D], at=over)
        cursor[0] = max(cursor[0], over[0])
        over = [at_xn]
        xrow = sb("xrow", [P, 2, XQ, D], at=over)
        assert over[0] <= start_o
        over = [start_o]
        share = sb("share", [P, PICKS, RT], at=over)
        share_hi = sb("share_hi", [P, PICKS, RT], F32R, at=over)
        share_lo = sb("share_lo", [P, PICKS, RT], F32R, at=over)
        pick = sb("pick", [P, PICKS, RT, E], at=over)
        total = sb("total", [P, E, A], at=over)
        upto = sb("upto", [P, E, A], at=over)
        more = sb("more", [P, E, BN], at=over)
        blocks = sb("blocks", [P, 3, E], at=over)
        pos_e = sb("pos_e", [P, A, E], at=over)
        pos = sb("pos", [P, A], at=over)
        pos_i = sb("pos_i", [P, A], I32, at=over)
        place_of = sb("place_of", [P, A], at=over)
        border = sb("border", [P, A], at=over)
        in_block = sb("in_block", [P, A, NB], at=over)
        at_place = sb("at_place", [P, A, P], F32R, at=over)
        entry = sb("entry", [P, A, 3, NB], F32R, at=over)
        table = sb("table", [P, 3, NB], at=over)
        tab = sb("tab", [P, 1, NB], at=over)
        shares = sb("shares", [P, NB], at=over)
        gather_u = sb("gather_u", [P, NB], U32, at=over)
        scatter_u = sb("scatter_u", [P, NB], U32, at=over)
        passed = sb("passed", [P, NB, E], at=over)
        owner = sb("owner", [P, NB], at=over)
        owner_i = sb("owner_i", [P, NB], I32, at=over)
        xg = [sb(f"xg{i}", [P, D], at=over) for i in range(XG)]
        xthi = [sb(f"xthi{i}", [P, D], F32R, at=over) for i in range(2)]
        xtlo = [sb(f"xtlo{i}", [P, D], F32R, at=over) for i in range(2)]
        hb = [sb(f"hb{i}", [P, FH], at=over) for i in range(2)]
        hr = [sb(f"hr{i}", [P, FH], at=over) for i in range(2)]
        yb = [sb(f"yb{i}", [P, D], at=over) for i in range(2)]
        ys = [sb(f"ys{i}", [P, D], at=over) for i in range(2)]
        assert over[0] <= end_o, (over[0], end_o)
        at_xc = cursor[0]
        xc = sb("xc", [P, 2, DC, HALF])
        vT = nc.alloc_sbuf_tensor_at("vT", [P, TOK], F32, offset=at_xc)
        over = [start]
        gx = sb("gx", [P, DC, TOK], at=over)
        gq, ga, gsum, gprod = (sb(n, [P, TOK], at=over) for n in ("gq", "ga", "gsum", "gprod"))
        gk = [sb(f"gk{i}", [P, TOK], at=over) for i in range(2)]
        gv = [sb(f"gv{i}", [P, TOK], at=over) for i in range(2)]
        head_sum = sb("head_sum", [P, P], at=over)
        assert over[0] <= pb_end
        assert cursor[0] <= nc.sbuf_usable_end, cursor[0]

        ps = ctx.enter_context(nc.psum_tensor("ps", [P, 8, 512], F32))

        def slot(k, n=GT):
            return ps[:, 2 * k:2 * k + 2, 0:n]

        def half(t, c, lead=()):
            return t[(slice(None),) + lead + (slice(c * HALF, (c + 1) * HALF),)].rearrange(
                "p (j n) -> p j n", j=2)

        def banks(t):
            return t.rearrange("p (j n) -> p j n", j=2)

        def squares(c):
            return oT[:, DC * c:DC * (c + 1), 0:HALF]

        def rstd(c):
            return oT[:, 2 * DC + c, 0:HALF]

        def deviation_at(c):
            return oT[:, 2 * DC + 2 + c, 0:HALF]

        def squares_of(g):
            return oT[:, DC * (g % 2):DC * (g % 2 + 1), 0:GT]

        def rstd_of(g):
            return oT[:, 2 * DC + g % 2, 0:GT]

        def centred(g):
            return xc[:, g // 2, :, (g % 2) * GT:(g % 2 + 1) * GT]

        def std_of(g):
            return oT[:, 2 * DC + 2 + g % 2, 0:GT]

        def group(t, g):
            return t[:, :, g * GT:(g + 1) * GT]

        s_idx_in, s_idx, s_gath = sem("s_idx_in"), sem("s_idx"), sem("s_gath")
        s_emb_in = [sem(f"s_emb_in{i}") for i in range(EP + 1)]
        s_wr, s_wo, s_wg = sem("s_wr"), sem("s_wo"), sem("s_wg")
        s_const = sem("s_const")
        s_gt_mm, s_gt = sem("s_gt_mm"), sem("s_gt")
        s_patch_mm, s_text_mm, s_emb, s_txt = sem("s_patch_mm"), sem("s_text_mm"), sem("s_emb"), sem("s_txt")
        s_mean, s_xc, s_sq, s_var, s_std = sem("s_mean"), sem("s_xc"), sem("s_sq"), sem("s_var"), sem("s_std")
        s_rstd, s_xn, s_xnhi, s_xnlo = sem("s_rstd"), sem("s_xn"), sem("s_xnhi"), sem("s_xnlo")
        s_wload = [sem("s_wload0"), sem("s_wload1")]
        s_whi, s_wlo = sem("s_whi"), sem("s_wlo")
        s_proj, s_exp, s_u, s_scan, s_ku = sem("s_proj"), sem("s_exp"), sem("s_u"), sem("s_scan"), sem("s_ku")
        s_uok, s_qraw, s_a, s_qa = sem("s_uok"), sem("s_qraw"), sem("s_a"), sem("s_qa")
        s_vt, s_vmm, s_v, s_pmm, s_p, s_omm, s_o = (sem(n) for n in ("s_vt", "s_vmm", "s_v", "s_pmm", "s_p", "s_omm", "s_o"))
        s_okcol, s_okmm, s_ok, s_way = sem("s_okcol"), sem("s_okmm"), sem("s_ok"), sem("s_way")
        s_womm, s_h2 = sem("s_womm"), sem("s_h2")
        s_rows_mm, s_rows, s_xrows, s_hrows = sem("s_rows_mm"), sem("s_rows"), sem("s_xrows"), sem("s_hrows")
        s_lgmm, s_lgt, s_lgtok, s_prob, s_exps = (sem(n) for n in ("s_lgmm", "s_lgt", "s_lgtok", "s_prob", "s_exps"))
        s_pick, s_count, s_share, s_off, s_place, s_entry, s_tabmm, s_owner, s_tab = (
            sem(n) for n in ("s_pick", "s_count", "s_share", "s_off", "s_place", "s_entry", "s_tabmm", "s_owner", "s_tab"))
        s_w1, s_w2, s_bias, s_w1hi, s_w1lo, s_xthi = (
            sem(n) for n in ("s_w1", "s_w2", "s_bias", "s_w1hi", "s_w1lo", "s_xthi"))
        s_gx = [sem(f"s_gx{i}") for i in range(XG)]
        s_tx, s_xt, s_up, s_hb, s_th, s_hr, s_dn, s_yb, s_ys, s_added = (
            sem(n) for n in ("s_tx", "s_xt", "s_up", "s_hb", "s_th", "s_hr", "s_dn", "s_yb", "s_ys", "s_added"))
        s_gw, s_gset, s_gproj, s_gread, s_gterm, s_gbc, s_gdone = (
            sem(n) for n in ("s_gw", "s_gset", "s_gproj", "s_gread", "s_gterm", "s_gbc", "s_gdone"))
        s_link, s_link2, s_first = sem("s_link"), sem("s_link2"), sem("s_first")

        block = ctx.enter_context(nc.Block())

        def early(n, count):
            return isinstance(n, int) and n < count

        def proj_done(hp, mat, c):
            return MATS * c + mat + 1 if early(hp, 1) else 2 * MATS * hp + 2 * mat + c + 1

        def proj_slot(hp, mat, c):
            return {GATE: 0, KEY: 1, QUERY: 3, VALUE: 2}[mat] if early(hp, 1) else c

        @block.sync
        def _(sp):
            sp.dma_start(idx_i[:], x_idx).then_inc(s_idx_in, 16)
            for i in range(EP):
                k = slice(i * PC // EP, (i + 1) * PC // EP)
                sp.dma_start(wtok[:, k], w_tok[:, k]).then_inc(s_emb_in[i], 16)
                sp.dma_start(pt[:, 0, k], patches[0, :, k]).then_inc(s_emb_in[i], 16)
                if i == 0:
                    sp.dma_start(wr[:], w_r).then_inc(s_wr, 16)
                    sp.dma_start(btok[:], b_tok).then_inc(s_wr, 16)
            sp.dma_start(pt[:, 1], patches[1]).then_inc(s_emb_in[EP], 16)
            for hp in range(HP):
                if hp >= 2:
                    sp.wait_ge(s_wlo, hp - 1)
                sp.dma_start(wraw[hp % 2][:], w_attn[hp]).then_inc(s_wload[hp % 2], 16)
                if hp == 1:
                    sp.dma_start(wo[:], w_o).then_inc(s_wo, 16)
                    sp.dma_start(wg[:], w_gate).then_inc(s_wg, 16)
            sp.dma_start(w1[:, 0:EARLY_W], w_1[:, 0:EARLY_W]).then_inc(s_w1, 16)
            sp.dma_start(b1[:], b_1).then_inc(s_bias, 16)
            sp.wait_ge(s_ok, 1)
            in_range = sp.value_load(ok_sum[0:1, 0:1], min_val=0, max_val=P)
            with sp.If(in_range < P):
                with sp.Fori(0, HP) as hp:
                    sp.wait_ge(s_gdone, hp + 1)
                    sp.dma_start(wraw[0][:], w_attn[bass.ds(hp, 1)].rearrange("o p n -> (o p) n")
                                 ).then_inc(s_gw, 16)
            sp.wait_ge(s_way, 1)
            sp.wait_ge(s_o, 4 * HP)
            sp.dma_start(w1[:, EARLY_W:], w_1[:, EARLY_W:]).then_inc(s_w1, 16)
            sp.dma_start(w2[:], w_2).then_inc(s_w2, 16)
            sp.dma_start(b2[:], b_2.to_broadcast([P, E * D])).then_inc(s_bias, 16)

            def rows(dram, t, c, done):
                at = c * HALF
                sp.dma_start(dram[at:at + (XQ - 1) * P].rearrange("(q p) d -> p q d", p=P), t[:, c, 0:XQ - 1]
                             ).then_inc(done, 16)
                sp.dma_start(dram[at + (XQ - 1) * P:at + HALF], t[0:XTAIL, c, XQ - 1]).then_inc(done, 16)

            for n, (dram, t, c, done) in enumerate(((out, hrow, 0, s_hrows), (out, hrow, 1, s_hrows),
                                                    (xrows, xrow, 0, s_xrows), (xrows, xrow, 1, s_xrows))):
                sp.wait_ge(s_rows, n + 1)
                rows(dram, t, c, done)
            sp.dma_start(out[TOK:TOK + P], hrow[:, 0, 0]).then_inc(s_hrows, 16)
            sp.wait_ge(s_xrows, 64)
            sp.wait_ge(s_hrows, 80)
            sp.wait_ge(s_added, 16 * NB)

        def three(pe, outs, pairs):
            for n, dst in enumerate(outs):
                for i, (shi, slo, mhi, mlo) in enumerate(pairs):
                    pe.matmul(dst, slo, mhi[n], start=(i == 0), stop=False)
                    pe.matmul(dst, shi, mlo[n], start=False, stop=False)
                    last = pe.matmul(dst, shi, mhi[n], start=False, stop=(i == len(pairs) - 1))
            return last

        @block.tensor
        def _(pe):
            def embed_patches(c):
                for k in range(PC):
                    if c == 0 and k % (PC // EP) == 0:
                        pe.wait_ge(s_emb_in[k // (PC // EP)], 32)
                    if c == 1 and k == 0:
                        pe.wait_ge(s_emb_in[EP], 16)
                    for m in range(DC):
                        last = pe.matmul(ps[:, 4 * c + m, 0:HB * NP], wtok[:, k, m * P:(m + 1) * P],
                                         pt[:, c, k, :], start=(k == 0), stop=(k == PC - 1))
                last.then_inc(s_patch_mm, 1)

            def embed_text(c):
                if c == 0:
                    pe.wait_ge(s_const, 5)
                    pe.wait_ge(s_gath, 16 * G)
                    for g in range(G):
                        last = pe.transpose(ps[:, 7, g * P:(g + 1) * P], gath[:, g, :], ident[:])
                    last.then_inc(s_gt_mm, 1)
                    pe.wait_ge(s_gt, 1)
                    pe.wait_ge(s_wr, 32)
                for m in range(DC):
                    last = pe.matmul(ps[:, 4 * c + 2 + m, 0:HB * NT], wr[:, m * P:(m + 1) * P],
                                     gT[:, c * HB * NT:(c + 1) * HB * NT], start=True, stop=True)
                last.then_inc(s_text_mm, 1)

            def mean(c):
                pe.wait_ge(s_emb, c + 1)
                pe.wait_ge(s_txt, c + 1)
                for j in range(2):
                    for m in range(DC):
                        last = pe.matmul(ps[:, 4 * c + j, 0:GT], mean_w[:], half(hT, c, (m,))[:, j, :],
                                         start=(m == 0), stop=(m == DC - 1))
                last.then_inc(s_mean, 1)

            def variance(c):
                pe.wait_ge(s_sq, c + 1)
                for j in range(2):
                    for m in range(DC):
                        last = pe.matmul(ps[:, 4 * c + j, 0:GT], mean_w[:], banks(squares(c)[:, m, :])[:, j, :],
                                         start=(m == 0), stop=(m == DC - 1))
                last.then_inc(s_var, 1)

            def project(hp, par, mat, c):
                k = proj_slot(hp, mat, c)
                pairs = [(whi[par][:, mat, m, :], wlo[par][:, mat, m, :],
                          [half(xnhi, c, (m,))[:, j, :] for j in range(2)],
                          [half(xnlo, c, (m,))[:, j, :] for j in range(2)]) for m in range(DC)]
                three(pe, [ps[:, 2 * k + j, 0:GT] for j in range(2)], pairs).then_inc(s_proj, 1)

            def first_projections():
                pe.wait_ge(s_wlo, 1)
                pe.wait_ge(s_xnlo, 1)
                project(0, 0, GATE, 0)
                project(0, 0, KEY, 0)
                project(0, 0, QUERY, 0)
                pe.wait_ge(s_std, 2)
                project(0, 0, VALUE, 0)
                pe.wait_ge(s_xnlo, 2)
                for mat, read in ((GATE, s_exp), (KEY, s_ku), (QUERY, s_qraw), (VALUE, s_vt)):
                    pe.wait_ge(read, 1)
                    project(0, 0, mat, 1)

            def projections(hp, par):
                pe.wait_ge(s_wlo, hp + 1)
                pe.wait_ge(s_qraw, 2 * hp)
                pe.wait_ge(s_vt, 2 * hp)
                pe.wait_ge(s_ku, 2 * hp)
                project(hp, par, GATE, 0)
                if early(hp, 2):
                    turn_values(0, 1)
                project(hp, par, GATE, 1)
                if early(hp, 2):
                    turn_values(0, 2)
                pair_scores(hp - 1, 1 - par, 0)
                if early(hp, 2):
                    turn_values(0, 3)
                for c in range(2):
                    pe.wait_ge(s_exp, 2 * hp + 1 + c)
                    project(hp, par, KEY, c)
                for c in range(2):
                    pe.wait_ge(s_ku, 2 * hp + 1 + c)
                    project(hp, par, QUERY, c)
                for c in range(2):
                    pe.wait_ge(s_qraw, 2 * hp + 1 + c)
                    project(hp, par, VALUE, c)

            def turn_values(hp, g):
                pe.wait_ge(s_vt, 2 * hp + 1 + g // 2)
                if not (early(hp, 1) and g == 0):
                    pe.wait_ge(s_v, 4 * hp + g)
                for b in range(GB):
                    t = slice((GB * g + b) * T, (GB * g + b + 1) * T)
                    last = pe.transpose(ps[0:T, 6, b * P:(b + 1) * P], vT[:, t], ident[:])
                last.then_inc(s_vmm, 1)

            def pair_scores(a, par, g, bank=4):
                pe.wait_ge(s_qa, 2 * a + 1 + g // 2)
                if early(a, HP) and a == HP - 1 and g:
                    pe.wait_ge(s_p, 4 * a + g - 1)
                    pe.wait_ge(s_vt, 2 * HP)
                elif not (early(a, 1) and g == 0):
                    pe.wait_ge(s_p, 4 * a + g)
                for h in range(2):
                    rows = slice(DK * h, DK * (h + 1))
                    for b in range(GB):
                        t = slice((GB * g + b) * T, (GB * g + b + 1) * T)
                        last = pe.matmul(ps[0:T, bank + h, b * T:(b + 1) * T], kU[par][rows, t], qA[par][rows, t],
                                         start=True, stop=True)
                last.then_inc(s_pmm, 1)

            def mix(a, par, g, bank=7):
                pe.wait_ge(s_p, 4 * a + g + 1)
                pe.wait_ge(s_v, 4 * a + g + 1)
                if early(a, HP) and a == HP - 1 and g:
                    pe.wait_ge(s_o, 4 * a + g - 1)
                    pe.wait_ge(s_v, 4 * HP)
                elif not (early(a, 1) and g == 0):
                    pe.wait_ge(s_o, 4 * a + g)
                for b in range(GB):
                    for h in range(2):
                        last = pe.matmul(ps[DK * h:DK * (h + 1), bank, b * T:(b + 1) * T],
                                         vb[par][0:T, GB * g + b, DK * h:DK * (h + 1)],
                                         pb[g % 2][0:T, h, b * T:(b + 1) * T], start=True, stop=True)
                last.then_inc(s_omm, 1)

            def pair_step(hp, par):
                projections(hp, par)
                for g in range(G):
                    turn_values(hp, g)
                    if g + 1 < G:
                        pair_scores(hp - 1, 1 - par, g + 1)
                    mix(hp - 1, 1 - par, g)

            embed_patches(0)
            embed_patches(1)
            embed_text(0)
            embed_text(1)
            mean(0)
            mean(1)
            variance(0)
            variance(1)
            first_projections()
            pe.wait_ge(s_qraw, 2)
            turn_values(0, 0)
            pair_step(1, 1)
            with pe.Fori(2, HP, 2) as i:
                pair_step(i, 0)
                pair_step(i + 1, 1)
            pe.wait_ge(s_okcol, 1)
            pe.matmul(ps[0:1, 0, 0:1], ok_col[:, 0:1], ones[:, 0:1], start=True, stop=True).then_inc(s_okmm, 1)
            for g in range(G):
                pair_scores(HP - 1, 1, g, bank=4 - 2 * (g % 2))
                if g:
                    mix(HP - 1, 1, g - 1, bank=7 - (g - 1) % 2)
            mix(HP - 1, 1, G - 1, bank=7 - (G - 1) % 2)

            def general():
                with pe.Fori(0, HP) as hp:
                    pe.wait_ge(s_gw, 16 * hp + 16)
                    pe.wait_ge(s_gdone, hp + 1)
                    for mat in range(MATS):
                        pe.wait_ge(s_gread, 4 * hp + mat + 1)
                        for c in range(2):
                            for j in range(2):
                                for m in range(DC):
                                    w = wraw[0][:, (mat * DC + m) * P:(mat * DC + m + 1) * P]
                                    last = pe.matmul(ps[:, 2 * c + j, 0:GT], w, half(gx, c, (m,))[:, j, :],
                                                     start=(m == 0), stop=(m == DC - 1))
                        last.then_inc(s_gproj, 1)
                    with pe.Fori(0, T) as d:
                        pe.wait_ge(s_gterm, T * hp + d + 1)
                        for c in range(2):
                            for j in range(2):
                                last = pe.matmul(ps[:, 2 * c + j, 0:GT], head_sum[:], half(gprod, c)[:, j, :],
                                                 start=True, stop=True)
                        last.then_inc(s_gbc, 1)

            pe.wait_ge(s_ok, 1)
            in_range = pe.value_load(ok_sum[0:1, 0:1], min_val=0, max_val=P)
            with pe.If(in_range < P):
                general()

            def out_projection(g, m):
                if g >= 2:
                    pe.wait_ge(s_h2, 2 * (g - 2) + m + 1)
                if m == 0 and g >= 1:
                    pe.wait_ge(s_o, 4 * (HP - 1) + g + 1)
                for a in range(HP):
                    last = pe.matmul(ps[:, 2 * (g % 2) + m, 0:GT], wo[:, a, m * P:(m + 1) * P],
                                     oT[:, a, g * GT:(g + 1) * GT], start=(a == 0), stop=(a == HP - 1))
                last.then_inc(s_womm, 1)

            def mean_of(g):
                pe.wait_ge(s_h2, 2 * (g + 1))
                if g >= 2:
                    pe.wait_ge(s_std, 2 + g - 1)
                for m in range(DC):
                    last = pe.matmul(ps[:, 4 + g % 2, 0:GT], mean_w[:], group(hT, g)[:, m, :],
                                     start=(m == 0), stop=(m == DC - 1))
                last.then_inc(s_mean, 1)

            def variance_of(g):
                pe.wait_ge(s_sq, 2 + g + 1)
                for m in range(DC):
                    last = pe.matmul(ps[:, 4 + g % 2, 0:GT], mean_w[:], squares_of(g)[:, m, :],
                                     start=(m == 0), stop=(m == DC - 1))
                last.then_inc(s_var, 1)

            def logits(g):
                pe.wait_ge(s_xn, 2 + g + 1)
                if g >= 2:
                    pe.wait_ge(s_lgt, g - 1)
                for m in range(DC):
                    last = pe.matmul(ps[0:E, 6 + g % 2, 0:GT], wg[:, m, :], centred(g)[:, m, :],
                                     start=(m == 0), stop=(m == DC - 1))
                last.then_inc(s_lgmm, 1)

            pe.wait_ge(s_wo, 16)
            pe.wait_ge(s_wg, 16)
            pe.wait_ge(s_o, 4 * (HP - 1) + 1)
            pe.wait_ge(s_p, 4 * HP)
            pe.wait_ge(s_way, 1)
            out_projection(0, 0)
            out_projection(0, 1)
            out_projection(1, 0)
            mean_of(0)
            out_projection(1, 1)
            variance_of(0)
            out_projection(2, 0)
            mean_of(1)
            out_projection(2, 1)
            variance_of(1)
            out_projection(3, 0)
            mean_of(2)
            logits(0)
            out_projection(3, 1)
            variance_of(2)
            mean_of(3)
            logits(1)

            def turn_rows(n, src, c, banks3):
                for q in range(XQ):
                    w = P if q < XQ - 1 else XTAIL
                    for m in range(DC):
                        t0 = (0 if src is xc else c * HALF) + q * P
                        cols = src[:, c, m, t0:t0 + w] if src is xc else src[:, m, t0:t0 + w]
                        o = (q % 2) * D + m * P
                        last = pe.transpose(ps[0:w, banks3[q // 2], o:o + P], cols, ident[:])
                last.then_inc(s_rows_mm, 1)

            def turn_logits():
                pe.wait_ge(s_lgt, G)
                for r in range(RT):
                    t0 = min(r * P, TOK - P)
                    last = pe.transpose(ps[:, 4, r * E:(r + 1) * E], lgT[:, t0:t0 + P], ident[0:E, 0:E])
                last.then_inc(s_lgtok, 1)

            def turn_x(b, par, buf=None, count=None):
                if isinstance(b, int):
                    buf, count = b % XG, 16 * (b // XG + 1)
                pe.wait_ge(s_gx[buf], count)
                if not early(b, 2):
                    pe.wait_ge(s_xt, b - 1)
                for m in range(DC):
                    last = pe.transpose(ps[:, 7 * par, m * P:(m + 1) * P], xg[buf][:, m * P:(m + 1) * P], ident[:])
                last.then_inc(s_tx, 1)

            def expert_of(b):
                at = owner_i[0:1, b:b + 1] if isinstance(b, int) else owner_i[0:1, bass.ds(b, 1)]
                return pe.value_load(at, min_val=0, max_val=E - 1)

            def up(b, par):
                e = expert_of(b)
                pe.wait_ge(s_xt, b + 1)
                if not early(b, 2):
                    pe.wait_ge(s_hb, b - 1)
                for m in range(DC):
                    hi, lo = (t[:, bass.ds(e, 1), m * FH:(m + 1) * FH].rearrange("p o n -> p (o n)")
                              for t in (w1hi, w1lo))
                    xhi, xlo = xthi[par][:, m * P:(m + 1) * P], xtlo[par][:, m * P:(m + 1) * P]
                    pe.matmul(ps[:, 1 + par, :], xlo, hi, start=(m == 0), stop=False)
                    pe.matmul(ps[:, 1 + par, :], xhi, lo, start=False, stop=False)
                    last = pe.matmul(ps[:, 1 + par, :], xhi, hi, start=False, stop=(m == DC - 1))
                last.then_inc(s_up, 1)

            def turn_h(b, par):
                pe.wait_ge(s_hb, b + 1)
                if not early(b, 2):
                    pe.wait_ge(s_hr, b - 1)
                for j in range(FC):
                    last = pe.transpose(ps[:, 3 + par, j * P:(j + 1) * P], hb[par][:, j * P:(j + 1) * P], ident[:])
                last.then_inc(s_th, 1)

            def down(b, par):
                e = expert_of(b)
                pe.wait_ge(s_hr, b + 1)
                if not early(b, 2):
                    pe.wait_ge(s_yb, b - 1)
                for j in range(FC):
                    last = pe.matmul(ps[:, 5 + par, 0:D], hr[par][:, j * P:(j + 1) * P],
                                     w2[:, bass.ds(e, 1), j * D:(j + 1) * D].rearrange("p o n -> p (o n)"),
                                     start=(j == 0), stop=(j == FC - 1))
                last.then_inc(s_dn, 1)

            def block_step(b, par, buf=None, count=None):
                up(b + 1, 1 - par)
                turn_x(b + 2, par, buf, count)
                turn_h(b, par)
                down(b - 1, 1 - par)

            pe.wait_ge(s_h2, 2 * G)
            turn_rows(0, hT, 0, (0, 1, 2))
            variance_of(3)
            logits(2)
            logits(3)
            pe.wait_ge(s_std, 2 + G - 1)
            turn_logits()
            pe.wait_ge(s_rows, 1)
            turn_rows(1, hT, 1, (0, 1, 2))
            pe.wait_ge(s_lgt, G)
            turn_rows(2, xc, 0, (6, 7, 3))
            pe.wait_ge(s_rows, 2)
            turn_rows(3, xc, 1, (0, 1, 2))
            pe.wait_ge(s_const, 7)
            pe.wait_ge(s_pick, 1)
            picks = pick[:].rearrange("p i r e -> p (i r e)")
            pe.wait_ge(s_prob, 1)
            pe.matmul(ps[:, 4, 0:A * E], tri[:], picks, start=True, stop=True)
            pe.wait_ge(s_std, 2 + G)
            pe.matmul(ps[:, 5, 0:A * E], mean_w[:], picks, start=True, stop=True).then_inc(s_count, 1)
            pe.wait_ge(s_rows, 3)
            for a in range(A):
                if a % RT == 0:
                    pe.wait_ge(s_place, a // RT + 1)
                    pe.wait_ge(s_entry, a // RT + 1)
                last = pe.matmul(ps[:, 6, 0:3 * NB], at_place[:, a, :], entry[:, a].rearrange("p v b -> p (v b)"),
                                 start=(a == 0), stop=(a == A - 1))
            last.then_inc(s_tabmm, 1)
            pe.wait_ge(s_owner, 1)
            pe.wait_ge(s_w1lo, E)
            pe.wait_ge(s_w2, 16)
            pe.wait_ge(s_rows, 4)
            turn_x(0, 0)
            turn_x(1, 1)
            up(0, 0)
            up(1, 1)
            turn_x(2, 0)
            turn_h(0, 0)
            block_step(1, 1)
            block_step(2, 0)
            with pe.Fori(0, (NB - 6) // UNROLL) as i:
                for k in range(UNROLL):
                    block_step(UNROLL * i + 3 + k, (3 + k) % 2, (5 + k) % XG, 32 * i + 16 * ((5 + k) // XG + 1))
            block_step(NB - 3, 1)
            up(NB - 1, 1)
            turn_h(NB - 2, 0)
            down(NB - 3, 1)
            turn_h(NB - 1, 1)
            down(NB - 2, 0)
            down(NB - 1, 1)

        @block.scalar
        def _(act):
            def embed_patches(c):
                act.wait_ge(s_patch_mm, c + 1)
                for m in range(DC):
                    last = act.activation(
                        hT[:, m, c * HALF:(c + 1) * HALF].rearrange("p (b t) -> p b t", t=T)[:, :, 0:NP],
                        ps[:, 4 * c + m, 0:HB * NP].rearrange("p (b t) -> p b t", t=NP),
                        ACT.Identity, bias=btok[:, m:m + 1])
                last.then_inc(s_emb, 1)

            def square(c):
                act.wait_ge(s_xc, c + 1)
                act.activation(squares(c), xc[:, c], ACT.Square).then_inc(s_sq, 1)

            def deviation(c):
                act.wait_ge(s_var, c + 1)
                act.activation(banks(deviation_at(c)), slot(2 * c), ACT.Sqrt, bias=eps[:]).then_inc(s_std, 1)

            def split_stream(c):
                act.wait_ge(s_xn, c + 1)
                act.activation(xnhi[:, :, c * HALF:(c + 1) * HALF], xc[:, c], ACT.Copy).then_inc(s_xnhi, 1)

            def load_table(func):
                act.activation(warm[:], eps[:], func)

            def split_pair(hp, par, wload):
                act.wait_ge(s_wload[par], wload)
                if not early(hp, 2):
                    act.wait_ge(s_proj, 2 * MATS * (hp - 1))
                act.activation(whi[par][:].rearrange("p a b n -> p (a b n)"), wraw[par][:, 0:WA], ACT.Copy)
                act.activation(bneg[par][:], wraw[par][:, WA:WA + 1], ACT.Copy, scale=-1.0).then_inc(s_whi, 1)

            def evacuate_gate(hp, par, c):
                tok = slice(c * HALF, (c + 1) * HALF)
                act.wait_ge(s_whi, hp + 1)
                act.wait_ge(s_proj, proj_done(hp, GATE, c))
                if not early(hp, 1):
                    act.wait_ge(s_u, 2 * hp - 1 + c)
                act.activation(half(e_g, c), slot(proj_slot(hp, GATE, c)), ACT.Exp, bias=bneg[par][:], scale=-1.0
                               ).then_inc(s_exp, 1)
                act.wait_ge(s_exp, 2 * hp + 1 + c)
                if not early(hp, 1):
                    act.wait_ge(s_scan, 2 * hp - 1 + c)
                act.activation(u_g[:, tok].rearrange("p (b t) -> p b t", t=T)[:, :, 1:T],
                               e_g[:, tok].rearrange("p (b t) -> p b t", t=T)[:, :, 1:T],
                               ACT.Copy, bias=1.0).then_inc(s_u, 1)

            def evacuate_q(hp, c):
                act.wait_ge(s_proj, proj_done(hp, QUERY, c))
                if not early(hp, 1):
                    act.wait_ge(s_qa, 2 * hp - 1 + c)
                act.activation(half(qraw, c), slot(proj_slot(hp, QUERY, c)), ACT.Copy).then_inc(s_qraw, 1)

            def evacuate_vt(hp, c):
                act.wait_ge(s_proj, proj_done(hp, VALUE, c))
                if not early(hp, 1):
                    act.wait_ge(s_vmm, 4 * hp - 2 + 2 * c)
                act.activation(half(vT, c), slot(proj_slot(hp, VALUE, c)), ACT.Copy).then_inc(s_vt, 1)

            def evacuate_v(hp, par, g):
                act.wait_ge(s_vmm, 4 * hp + g + 1)
                if not early(hp, 2) and g == 0:
                    act.wait_ge(s_omm, 4 * hp - 4)
                act.activation(vb[par][0:T, GB * g:GB * (g + 1), :].rearrange("p b n -> p (b n)"), ps[0:T, 6, :], ACT.Copy).then_inc(s_v, 1)

            def evacuate_o(a, g, bank=7):
                act.wait_ge(s_omm, 4 * a + g + 1)
                act.activation(oT[:, bass.ds(a, 1), g * GT:(g + 1) * GT], ps[:, bank:bank + 1, 0:GT], ACT.Copy
                               ).then_inc(s_o, 1)

            def pair_step(hp, par, wload, tail=False):
                evacuate_gate(hp, par, 0)
                if early(hp, 2):
                    evacuate_v(0, 0, 1)
                evacuate_gate(hp, par, 1)
                if early(hp, 2):
                    evacuate_v(0, 0, 2)
                    evacuate_v(0, 0, 3)
                if not tail:
                    split_pair(hp + 1, 1 - par, wload)
                evacuate_q(hp, 0)
                evacuate_q(hp, 1)
                evacuate_vt(hp, 0)
                evacuate_vt(hp, 1)
                for g in range(G):
                    evacuate_v(hp, par, g)
                    evacuate_o(hp - 1, g)

            act.wait_ge(s_const, 4)
            load_table(ACT.Sqrt)
            act.wait_ge(s_wr, 32)
            embed_patches(0)
            embed_patches(1)
            split_pair(0, 0, 16)
            square(0)
            square(1)
            deviation(0)
            deviation(1)
            load_table(ACT.Exp)
            split_stream(0)
            evacuate_gate(0, 0, 0)
            split_stream(1)
            evacuate_q(0, 0)
            evacuate_vt(0, 0)
            evacuate_gate(0, 0, 1)
            split_pair(1, 1, 16)
            evacuate_q(0, 1)
            evacuate_vt(0, 1)
            evacuate_v(0, 0, 0)
            pair_step(1, 1, 32)
            with act.Fori(2, HP - 2, 2) as i:
                pair_step(i, 0, 8 * i + 16)
                pair_step(i + 1, 1, 8 * i + 32)
            pair_step(HP - 2, 0, 16 * (HP // 2))
            pair_step(HP - 1, 1, 0, tail=True)
            for g in range(G):
                evacuate_o(HP - 1, g, bank=7 - g % 2)

            def general():
                with act.Fori(0, HP) as hp:
                    act.wait_ge(s_gw, 16 * hp + 16)
                    act.wait_ge(s_gdone, hp + 1)
                    act.activation(bneg[0][:], wraw[0][:, WA:WA + 1], ACT.Copy, scale=-1.0).then_inc(s_gset, 1)
                    act.wait_ge(s_gset, hp + 1)
                    act.wait_ge(s_gproj, 4 * hp + 1)
                    for c in range(2):
                        last = act.activation(half(ga, c), slot(c), ACT.Exp, bias=bneg[0][:], scale=-1.0)
                    last.then_inc(s_gread, 1)

            act.wait_ge(s_ok, 1)
            in_range = act.value_load(ok_sum[0:1, 0:1], min_val=0, max_val=P)
            with act.If(in_range < P):
                general()

            def rows(n, t, c, banks3, tail):
                act.wait_ge(s_rows_mm, n + 1)
                act.activation(t[:, c, 0:4].rearrange("p (a q) d -> p a (q d)", a=2),
                               ps[:, banks3:banks3 + 2, :], ACT.Copy)
                act.activation(t[0:XTAIL, c, 4], ps[0:XTAIL, tail, 0:D], ACT.Copy).then_inc(s_rows, 1)

            def relu(b, par):
                at = owner_i[0:1, b:b + 1] if isinstance(b, int) else owner_i[0:1, bass.ds(b, 1)]
                e = act.value_load(at, min_val=0, max_val=E - 1)
                act.wait_ge(s_th, b + 1)
                if not early(b, 2):
                    act.wait_ge(s_dn, b - 1)
                for j in range(FC):
                    col = b1[:, bass.ds(e, 1), j:j + 1].rearrange("p o n -> p (o n)")
                    last = act.activation(hr[par][:, j * P:(j + 1) * P], ps[:, 3 + par, j * P:(j + 1) * P], ACT.Relu,
                                          bias=col)
                last.then_inc(s_hr, 1)

            def scale(b, par):
                act.wait_ge(s_yb, b + 1)
                if not early(b, 2):
                    act.wait_ge(s_added, 16 * b - 16)
                col = shares[:, b:b + 1] if isinstance(b, int) else shares[:, bass.ds(b, 1)]
                act.activation(ys[par][:], yb[par][:], ACT.Copy, scale=col).then_inc(s_ys, 1)

            load_table(ACT.Sqrt)

            def square_of(g):
                act.wait_ge(s_xc, 2 + g + 1)
                act.activation(squares_of(g), centred(g), ACT.Square).then_inc(s_sq, 1)

            def deviation_of(g):
                act.wait_ge(s_var, 2 + g + 1)
                act.activation(std_of(g), ps[:, 4 + g % 2, 0:GT], ACT.Sqrt, bias=eps[:]).then_inc(s_std, 1)

            def copy_logits(g):
                act.wait_ge(s_lgmm, g + 1)
                act.activation(lgT[:, g * GT:(g + 1) * GT], ps[0:E, 6 + g % 2, 0:GT], ACT.Copy).then_inc(s_lgt, 1)

            square_of(0)
            deviation_of(0)
            square_of(1)
            deviation_of(1)
            square_of(2)
            copy_logits(0)
            deviation_of(2)
            square_of(3)
            copy_logits(1)
            rows(0, hrow, 0, 0, 2)
            deviation_of(3)
            load_table(ACT.Exp)
            copy_logits(2)
            copy_logits(3)
            act.wait_ge(s_prob, 1)
            act.activation(pr[:], lg[:], ACT.Exp).then_inc(s_exps, 1)
            rows(1, hrow, 1, 0, 2)
            rows(2, xrow, 0, 6, 3)
            rows(3, xrow, 1, 0, 2)
            act.wait_ge(s_share, 1)
            act.activation(share_hi[:], share[:], ACT.Copy).then_inc(s_share, 1)
            act.wait_ge(s_owner, 1)
            act.wait_ge(s_bias, 32)
            act.wait_ge(s_tab, 3)
            relu(0, 0)
            relu(1, 1)
            scale(0, 0)
            relu(2, 0)
            scale(1, 1)
            with act.Fori(3, NB - 1, 2) as i:
                relu(i, 1)
                scale(i - 1, 0)
                relu(i + 1, 0)
                scale(i, 1)
            relu(NB - 1, 1)
            scale(NB - 2, 0)
            scale(NB - 1, 1)

        @block.vector
        def _(dve):
            links = [0]

            def link(ins):
                links[0] += 1
                ins.then_inc(s_link, 1)
                dve.wait_ge(s_link, links[0])

            dve.wait_ge(s_idx_in, 16)
            link(dve.tensor_copy(idx_f[:], idx_i[:]))
            link(dve.tensor_scalar(idx_n[:], idx_f[:], 0.0, float(VOCAB), ALU.is_lt, ALU.mult))
            link(dve.tensor_tensor(idx_f[:], idx_f[:], idx_n[:], ALU.add))
            dve.tensor_scalar(idx_u[:], idx_f[:], 0.0, float(VOCAB - 1), ALU.max, ALU.min).then_inc(s_idx, 1)
            dve.memset(u_ok[:], 1.0).then_inc(s_uok, 1)
            dve.wait_ge(s_gt_mm, 1)
            dve.tensor_copy(gT[:], ps[:, 7, :]).then_inc(s_gt, 1)

            def embed_text(c):
                dve.wait_ge(s_text_mm, c + 1)
                for m in range(DC):
                    last = dve.tensor_copy(
                        hT[:, m, c * HALF:(c + 1) * HALF].rearrange("p (b t) -> p b t", t=T)[:, :, NP:T],
                        ps[:, 4 * c + 2 + m, 0:HB * NT].rearrange("p (b t) -> p b t", t=NT))
                last.then_inc(s_txt, 1)

            def centre(c):
                dve.wait_ge(s_mean, c + 1)
                dve.wait_ge(s_emb, c + 1)
                dve.wait_ge(s_txt, c + 1)
                for m in range(DC):
                    last = dve.tensor_tensor(banks(xc[:, c, m, :]), half(hT, c, (m,)), slot(2 * c), ALU.subtract)
                last.then_inc(s_xc, 1)

            def normalise(c):
                dve.wait_ge(s_std, c + 1)
                dve.reciprocal(rstd(c), deviation_at(c)).then_inc(s_rstd, 1)
                dve.wait_ge(s_rstd, c + 1)
                dve.wait_ge(s_sq, c + 1)
                for m in range(DC):
                    last = dve.tensor_tensor(xc[:, c, m, :], xc[:, c, m, :], rstd(c), ALU.mult)
                last.then_inc(s_xn, 1)

            def split_stream(c):
                dve.wait_ge(s_xnhi, c + 1)
                tok = slice(c * HALF, (c + 1) * HALF)
                dve.tensor_tensor(xnlo[:, :, tok], xc[:, c], xnhi[:, :, tok].bitcast(F32), ALU.subtract
                                  ).then_inc(s_xnlo, 1)

            def decay(hp, par):
                for c in range(2):
                    dve.wait_ge(s_u, 2 * hp + c + 1)
                    if not early(hp, 1):
                        dve.wait_ge(s_a, 4 * hp - 2 + 2 * c)
                    dve.tensor_tensor_scan(U[:, c * HALF:(c + 1) * HALF], u_g[:, c * HALF:(c + 1) * HALF], first[:],
                                           1.0, ALU.mult, ALU.add).then_inc(s_scan, 1)
                    dve.wait_ge(s_scan, 2 * hp + c + 1)
                    dve.wait_ge(s_proj, proj_done(hp, KEY, c))
                    if c == 0 and not early(hp, 2):
                        dve.wait_ge(s_pmm, 4 * hp - 4)
                    dve.tensor_tensor(half(kU[par], c), slot(proj_slot(hp, KEY, c)), half(U, c), ALU.mult).then_inc(s_ku, 1)
                dve.wait_ge(s_uok, hp + 1)
                dve.scalar_tensor_tensor(u_ok[:], U[:].rearrange("p (b t) -> p b t", t=T)[:, :, T - 1], U_LIMIT,
                                         u_ok[:], ALU.is_le, ALU.mult).then_inc(s_uok, 1)

            def invert(hp, g):
                if not early(hp, 1):
                    dve.wait_ge(s_qa, 2 * hp - 1 + g // 2)
                dve.reciprocal(invU[:, g * GT:(g + 1) * GT], U[:, g * GT:(g + 1) * GT]).then_inc(s_a, 1)

            def mask(a, g, bank=4):
                dve.wait_ge(s_pmm, 4 * a + g + 1)
                if not (early(a, 1) and g < 2):
                    dve.wait_ge(s_omm, 4 * a + g - 1)
                dve.tensor_tensor(pb[g % 2][0:T].bitcast(U32), ps[0:T, bank:bank + 2, 0:GT].bitcast(U32), causal_bits[0:T],
                                  ALU.bitwise_and).then_inc(s_p, 1)

            def pair_step(hp, par):
                decay(hp, par)
                mask(hp - 1, 0)
                for g in range(3):
                    invert(hp, g)
                mask(hp - 1, 1)
                mask(hp - 1, 2)
                invert(hp, 3)
                mask(hp - 1, 3)

            embed_text(0)
            embed_text(1)
            centre(0)
            centre(1)
            normalise(0)
            split_stream(0)
            normalise(1)
            split_stream(1)
            dve.wait_ge(s_const, 6)
            dve.tensor_scalar(causal_bits[:].bitcast(I32), causal[:], -1.0, None, ALU.mult)
            dve.wait_ge(s_first, 1)
            decay(0, 0)
            for g in range(G):
                invert(0, g)
            pair_step(1, 1)
            with dve.Fori(2, HP, 2) as i:
                pair_step(i, 0)
                pair_step(i + 1, 1)
            dve.wait_ge(s_uok, HP + 1)
            dve.tensor_reduce(ok_col[:], u_ok[:], AX_X, ALU.min).then_inc(s_okcol, 1)
            dve.wait_ge(s_okmm, 1)
            dve.tensor_copy(ok_sum[:], ps[0:1, 0, 0:1]).then_inc(s_ok, 1)
            for g in range(G):
                mask(HP - 1, g, bank=4 - 2 * (g % 2))
            dve.wait_ge(s_ok, 1)

            def general():
                dve.wait_ge(s_o, 4 * HP)
                dve.wait_ge(s_qa, 2 * HP)
                dve.tensor_tensor(gx[:], xnhi[:].bitcast(F32), xnlo[:].bitcast(F32), ALU.add)
                dve.memset(head_sum[:], 0.0)
                dve.drain()
                dve.memset(head_sum[0:DK, 0:DK], 1.0)
                dve.memset(head_sum[DK:P, DK:P], 1.0).then_inc(s_gread, 1)
                dve.drain().then_inc(s_gdone, 1)

                def by_batch(t):
                    return t[:].rearrange("p (b t) -> p b t", t=T)

                with dve.Fori(0, HP) as hp:
                    for i, dst in ((KEY, gk[0]), (QUERY, gq), (VALUE, gv[0])):
                        dve.wait_ge(s_gproj, 4 * hp + i + 1)
                        for c in range(2):
                            last = dve.tensor_copy(half(dst, c), slot(c))
                        last.then_inc(s_gread, 1)
                    dve.tensor_scalar(ga[:], ga[:], 1.0, None, ALU.add)
                    dve.drain()
                    dve.reciprocal(ga[:], ga[:])
                    dve.memset(gsum[:], 0.0)
                    dve.drain()
                    with dve.Fori(0, T, 2) as d:
                        for i in range(2):
                            dve.tensor_tensor(gprod[:], gq[:], gk[i][:], ALU.mult).then_inc(s_gterm, 1)
                            dve.tensor_tensor(by_batch(gk[1 - i])[:, :, 1:T], by_batch(ga)[:, :, 1:T],
                                              by_batch(gk[i])[:, :, 0:T - 1], ALU.mult)
                            dve.memset(by_batch(gk[1 - i])[:, :, 0:1], 0.0)
                            dve.tensor_copy(by_batch(gv[1 - i])[:, :, 1:T], by_batch(gv[i])[:, :, 0:T - 1])
                            dve.memset(by_batch(gv[1 - i])[:, :, 0:1], 0.0)
                            dve.wait_ge(s_gbc, T * hp + d + i + 1)
                            for c in range(2):
                                dve.tensor_tensor(half(gprod, c), slot(c), half(gv[i], c), ALU.mult)
                            dve.drain()
                            dve.tensor_tensor(gsum[:], gsum[:], gprod[:], ALU.add)
                            dve.drain()
                    dve.tensor_copy(oT[:, bass.ds(hp, 1), :], gsum[:].unsqueeze(1))
                    dve.drain().then_inc(s_gdone, 1)

            in_range = dve.value_load(ok_sum[0:1, 0:1], min_val=0, max_val=P)
            with dve.If(in_range < P):
                general()
            dve.drain().then_inc(s_way, 1)

            def residual(g, m):
                dve.wait_ge(s_womm, 2 * g + m + 1)
                dve.tensor_tensor(group(hT, g)[:, m, :], group(hT, g)[:, m, :], ps[:, 2 * (g % 2) + m, 0:GT], ALU.add
                                  ).then_inc(s_h2, 1)

            def centre_of(g):
                dve.wait_ge(s_mean, 2 + g + 1)
                dve.wait_ge(s_h2, 2 * (g + 1))
                dve.tensor_tensor(centred(g), group(hT, g),
                                  ps[:, 4 + g % 2, 0:GT].unsqueeze(1).to_broadcast([P, DC, GT]), ALU.subtract
                                  ).then_inc(s_xc, 1)

            def normalise_of(g):
                dve.wait_ge(s_std, 2 + g + 1)
                dve.reciprocal(rstd_of(g), std_of(g)).then_inc(s_rstd, 1)
                dve.wait_ge(s_rstd, 2 + g + 1)
                dve.wait_ge(s_sq, 2 + g + 1)
                dve.tensor_tensor(centred(g), centred(g), rstd_of(g).unsqueeze(1).to_broadcast([P, DC, GT]), ALU.mult
                                  ).then_inc(s_xn, 1)

            residual(0, 0)
            residual(0, 1)
            residual(1, 0)
            centre_of(0)
            residual(1, 1)
            normalise_of(0)
            residual(2, 0)
            centre_of(1)
            residual(2, 1)
            normalise_of(1)
            residual(3, 0)
            centre_of(2)
            residual(3, 1)
            centre_of(3)
            normalise_of(2)
            normalise_of(3)

            def wide(t):
                return t.unsqueeze(2).to_broadcast([P, RT, E])

            logits = ps[:, 4, 0:RT * E].rearrange("p (r e) -> p r e", e=E)
            dve.wait_ge(s_const, 7)
            dve.wait_ge(s_lgtok, 1)
            link(dve.tensor_reduce(rs[:, 0, :], logits, AX_X, ALU.max))
            dve.tensor_tensor(lg[:], logits, wide(rs[:, 0, :]), ALU.subtract).then_inc(s_prob, 1)
            dve.wait_ge(s_exps, 1)
            link(dve.tensor_reduce(rs[:, 1, :], pr[:], AX_X, ALU.add))
            link(dve.reciprocal(rs[:, 1, :], rs[:, 1, :]))
            link(dve.tensor_tensor(pr[:], pr[:], wide(rs[:, 1, :]), ALU.mult))
            for r in range(RT):
                last = dve.max(top[:, r, :], pr[:, r, :])
            link(last)
            for r in range(RT):
                last = dve.max_index(topi[:, r, :], top[:, r, :], pr[:, r, :])
            link(last)
            link(dve.tensor_copy(topf[:], topi[:]))

            def by_pick(t):
                return t[:, :, 0:PICKS].rearrange("p r i -> p i r")

            dve.tensor_tensor(pick[:], expert_no[:],
                              by_pick(topf).unsqueeze(3).to_broadcast([P, PICKS, RT, E]), ALU.is_equal
                              ).then_inc(s_pick, 1)
            link(dve.tensor_tensor(rs[:, 2, :], top[:, :, 0], top[:, :, 1], ALU.add))
            link(dve.reciprocal(rs[:, 2, :], rs[:, 2, :]))
            link(dve.tensor_tensor(share[:], by_pick(top),
                                   rs[:, 2, :].unsqueeze(1).to_broadcast([P, PICKS, RT]), ALU.mult))
            dve.memset(share[0:DUP, :, RT - 1], 0.0).then_inc(s_share, 1)
            dve.wait_ge(s_share, 2)
            dve.tensor_tensor(share_lo[:], share[:], share_hi[:].bitcast(F32), ALU.subtract).then_inc(s_share, 1)

            flat = "p e a -> p (e a)"
            dve.wait_ge(s_count, 1)
            link(dve.tensor_scalar(total[:], ps[:, 5, 0:A * E].rearrange("p (a e) -> p e a", e=E), float(D), None,
                                   ALU.mult))
            link(dve.tensor_tensor_scan(upto[:].rearrange(flat), seg[:].rearrange(flat), total[:].rearrange(flat),
                                        0.0, ALU.mult, ALU.add))
            link(dve.tensor_tensor(more[:], upto[:, :, A - 1:A].to_broadcast([P, E, BN]), steps[:], ALU.is_gt))
            link(dve.tensor_reduce(blocks[:, 0, :], more[:], AX_X, ALU.add))
            link(dve.tensor_tensor_scan(blocks[:, 1, :], ones_e[:], blocks[:, 0, :], 0.0, ALU.mult, ALU.add))
            link(dve.tensor_tensor(blocks[:, 1, :], blocks[:, 1, :], blocks[:, 0, :], ALU.subtract))
            link(dve.tensor_tensor(upto[:], upto[:], total[:], ALU.subtract))
            link(dve.scalar_tensor_tensor(upto[:], blocks[:, 1, :].unsqueeze(2).to_broadcast([P, E, A]), float(P),
                                          upto[:], ALU.mult, ALU.add))
            link(dve.tensor_tensor(pos_e[:], ps[:, 4, 0:A * E].rearrange("p (a e) -> p a e", e=E),
                                   upto[:].rearrange("p e a -> p a e"), ALU.add))
            dve.wait_ge(s_pick, 1)
            link(dve.tensor_tensor(pos_e[:], pos_e[:], pick[:].rearrange("p i r e -> p (i r) e"), ALU.mult))
            link(dve.tensor_reduce(pos[:], pos_e[:], AX_X, ALU.add))
            link(dve.tensor_copy(pos_i[:], pos[:]))
            link(dve.tensor_scalar(pos_i[:], pos_i[:], P - 1, None, ALU.bitwise_and))
            link(dve.tensor_copy(place_of[:], pos_i[:]))
            link(dve.tensor_tensor(border[:], pos[:], place_of[:], ALU.subtract))
            dve.tensor_tensor(in_block[:], block_start[:].unsqueeze(1).to_broadcast([P, A, NB]),
                              border[:].unsqueeze(2).to_broadcast([P, A, NB]), ALU.is_equal).then_inc(s_off, 1)
            for i in range(PICKS):
                a = slice(i * RT, (i + 1) * RT)
                dve.tensor_tensor(at_place[:, a], place[:].unsqueeze(1).to_broadcast([P, RT, P]),
                                  place_of[:, a].unsqueeze(2).to_broadcast([P, RT, P]), ALU.is_equal
                                  ).then_inc(s_place, 1)
            link(dve.tensor_tensor(passed[:], blocks[:, 1, :].unsqueeze(1).to_broadcast([P, NB, E]), block_no[:],
                                   ALU.is_le))
            link(dve.tensor_reduce(owner[:], passed[:], AX_X, ALU.add))
            dve.tensor_scalar(owner_i[:], owner[:], -1.0, None, ALU.add).then_inc(s_owner, 1)
            dve.wait_ge(s_tabmm, 1)
            link(dve.tensor_copy(table[:], ps[:, 6, 0:3 * NB].rearrange("p (v b) -> p v b", b=NB)))
            dve.tensor_scalar(gather_u[:], table[:, 0, :], -1.0, 0.0, ALU.add, ALU.max).then_inc(s_tab, 1)
            link(dve.tensor_scalar(tab[:, 0, :], table[:, 0, :], 0.5, None, ALU.is_lt))
            link(dve.tensor_scalar(tab[:, 0, :], tab[:, 0, :], spare_no[:], -1.0, ALU.mult, ALU.add))
            dve.tensor_tensor(scatter_u[:], table[:, 0, :], tab[:, 0, :], ALU.add).then_inc(s_tab, 1)
            dve.tensor_tensor(shares[:], table[:, 1, :], table[:, 2, :], ALU.add).then_inc(s_tab, 1)

            def copy_x(b, par):
                dve.wait_ge(s_tx, b + 1)
                if not early(b, 2):
                    dve.wait_ge(s_up, b - 1)
                dve.tensor_copy(xthi[par][:], ps[:, 7 * par, 0:D]).then_inc(s_xthi, 1)
                dve.wait_ge(s_xthi, b + 1)
                dve.tensor_tensor(xtlo[par][:], ps[:, 7 * par, 0:D], xthi[par][:].bitcast(F32), ALU.subtract
                                  ).then_inc(s_xt, 1)

            def owner_of(b):
                at = owner_i[0:1, b:b + 1] if isinstance(b, int) else owner_i[0:1, bass.ds(b, 1)]
                return dve.value_load(at, min_val=0, max_val=E - 1)

            def copy_h(b, par):
                dve.wait_ge(s_up, b + 1)
                if not early(b, 2):
                    dve.wait_ge(s_th, b - 1)
                dve.tensor_copy(hb[par][:], ps[:, 1 + par, :]).then_inc(s_hb, 1)

            def add_b2(b, par):
                e = owner_of(b)
                dve.wait_ge(s_dn, b + 1)
                if not early(b, 2):
                    dve.wait_ge(s_ys, b - 1)
                dve.tensor_tensor(yb[par][:], ps[:, 5 + par, 0:D],
                                  b2[:, bass.ds(e, 1), :].rearrange("p o n -> p (o n)"), ALU.add
                                  ).then_inc(s_yb, 1)

            def block_step(b, par):
                copy_h(b + 1, 1 - par)
                copy_x(b + 2, par)
                add_b2(b - 1, 1 - par)

            dve.wait_ge(s_owner, 1)
            dve.wait_ge(s_bias, 32)
            copy_x(0, 0)
            copy_x(1, 1)
            copy_h(0, 0)
            copy_h(1, 1)
            copy_x(2, 0)
            block_step(1, 1)
            block_step(2, 0)
            with dve.Fori(3, NB - 3, 2) as i:
                block_step(i, 1)
                block_step(i + 1, 0)
            block_step(NB - 3, 1)
            copy_h(NB - 1, 1)
            add_b2(NB - 3, 1)
            add_b2(NB - 2, 0)
            add_b2(NB - 1, 1)

        @block.gpsimd
        def _(pool):
            pool.memset(ident[:], 0.0).then_inc(s_const, 1)
            pool.memset(mean_w[:], 1.0 / D).then_inc(s_const, 1)
            pool.memset(eps[:], LN_EPS).then_inc(s_const, 1)
            pool.memset(ones[:], 1.0).then_inc(s_const, 1)
            pool.wait_ge(s_const, 4)
            pool.affine_select(out=ident[:], in_=ident[:], compare_op=ALU.not_equal, fill=1.0, base=0,
                               pattern=[[-1, P]], channel_multiplier=1).then_inc(s_const, 1)
            pool.wait_ge(s_idx, 1)
            for g in range(G):
                pool.indirect_dma_start(out=gath[:, g, :], out_offset=None, in_=w_l,
                                        in_offset=bass.IndirectOffsetOnAxis(ap=idx_u[:, g:g + 1], axis=0),
                                        bounds_check=VOCAB - 1).then_inc(s_gath, 16)
            pool.memset(first[:], 0.0)
            pool.memset(causal[:], 1.0).then_inc(s_link2, 1)
            pool.wait_ge(s_link2, 1)
            pool.memset(first[:].rearrange("p (b t) -> p b t", t=T)[:, :, 0:1], 1.0)
            keep = causal[:].rearrange("p h (b t) -> p (h b) t", t=T)
            pool.affine_select(out=keep, in_=keep, compare_op=ALU.is_ge, fill=0.0, base=0,
                               pattern=[[0, 2 * GB], [1, T]], channel_multiplier=-1).then_inc(s_const, 1)

            def split_pair(hp, par):
                pool.wait_ge(s_whi, hp + 1)
                pool.tensor_tensor(wlo[par][:].rearrange("p a b n -> p (a b n)"), wraw[par][:, 0:WA],
                                   whi[par][:].bitcast(F32).rearrange("p a b n -> p (a b n)"), ALU.subtract
                                   ).then_inc(s_wlo, 1)

            def scale_q(hp, par):
                for c in range(2):
                    pool.wait_ge(s_qraw, 2 * hp + 1 + c)
                    pool.wait_ge(s_a, 4 * hp + 2 + 2 * c)
                    if c == 0 and not early(hp, 2):
                        pool.wait_ge(s_pmm, 4 * hp - 4)
                    tok = slice(c * HALF, (c + 1) * HALF)
                    pool.tensor_tensor(qA[par][:, tok], qraw[:, tok], invU[:, tok], ALU.mult).then_inc(s_qa, 1)

            def pair_step(hp, par, tail=False):
                if not tail:
                    split_pair(hp + 1, 1 - par)
                scale_q(hp, par)

            split_pair(0, 0)
            pool.memset(u_g[:].rearrange("p (b t) -> p b t", t=T)[:, :, 0:1], 0.0).then_inc(s_first, 1)
            split_pair(1, 1)
            scale_q(0, 0)
            pair_step(1, 1)
            with pool.Fori(2, HP - 2, 2) as i:
                pair_step(i, 0)
                pair_step(i + 1, 1)
            pair_step(HP - 2, 0)
            pair_step(HP - 1, 1, tail=True)

            def iota(t, pattern, base, step=0):
                return pool.iota(t, pattern=pattern, base=base, channel_multiplier=step,
                                 allow_small_or_imprecise_dtypes=True)

            iota(expert_no[:], [[0, PICKS], [0, RT], [1, E]], 0)
            iota(steps[:], [[0, E], [P, BN]], 0)
            iota(block_start[:], [[P, NB]], 0)
            iota(block_no[:], [[1, NB], [0, E]], 0)
            iota(place[:], [[1, P]], 0)
            iota(row_no[:, :, 0:RT - 1], [[0, PICKS], [P, RT - 1]], 1, 1)
            iota(row_no[:, :, RT - 1:RT], [[0, PICKS], [0, 1]], TOK - P + 1, 1)
            iota(spare_no[:], [[0, 1]], TOK + 1, 1)
            pool.memset(ones_e[:], 1.0)
            pool.memset(seg[:], 1.0)
            pool.memset(tri[:], 1.0).then_inc(s_link2, 1)
            pool.wait_ge(s_link2, 2)
            pool.memset(seg[:, :, 0:1], 0.0)
            pool.memset(steps[:, :, 0:1], -1.0)
            pool.memset(row_no[0:DUP, :, RT - 1:RT], 0.0)
            pool.memset(expert_no[0:DUP, :, RT - 1, :], -1.0)
            pool.affine_select(out=tri[:], in_=tri[:], compare_op=ALU.is_gt, fill=0.0, base=0,
                               pattern=[[1, P]], channel_multiplier=-1).then_inc(s_const, 1)
            pool.wait_ge(s_way, 1)
            pool.wait_ge(s_o, 4 * HP)
            pool.wait_ge(s_w1, 32)
            for e in range(E):
                pool.tensor_copy(w1hi[:, e], w1[:, e]).then_inc(s_w1hi, 1)
                pool.wait_ge(s_w1hi, e + 1)
                pool.tensor_tensor(w1lo[:, e], w1[:, e], w1hi[:, e].bitcast(F32), ALU.subtract).then_inc(s_w1lo, 1)
            pool.wait_ge(s_off, 1)
            pool.wait_ge(s_share, 3)
            pool.wait_ge(s_const, 7)

            for i in range(PICKS):
                a = slice(i * RT, (i + 1) * RT)
                for v, t in enumerate((row_no, share_hi, share_lo)):
                    t = t[:, i] if v == 0 else t[:, i].bitcast(F32)
                    last = pool.tensor_tensor(entry[:, a, v, :], in_block[:, a],
                                              t.unsqueeze(2).to_broadcast([P, RT, NB]), ALU.mult)
                last.then_inc(s_entry, 1)

            def gather(b):
                if b >= XG:
                    pool.wait_ge(s_tx, b - XG + 1)
                pool.indirect_dma_start(out=xg[b % XG][:], out_offset=None, in_=xrows,
                                        in_offset=bass.IndirectOffsetOnAxis(ap=gather_u[:, b:b + 1], axis=0),
                                        bounds_check=TOK - 1).then_inc(s_gx[b % XG], 16)

            def scatter(b):
                if b >= 1:
                    pool.wait_ge(s_added, 16 * b)
                pool.wait_ge(s_ys, b + 1)
                pool.indirect_dma_start(out=out,
                                        out_offset=bass.IndirectOffsetOnAxis(ap=scatter_u[:, b:b + 1], axis=0),
                                        in_=ys[b % 2][:], in_offset=None, bounds_check=TOK + P - 1,
                                        compute_op=ALU.add).then_inc(s_added, 16)

            pool.wait_ge(s_tab, 1)
            pool.wait_ge(s_xrows, 64)
            for b in range(XG + 2):
                gather(b)
            pool.wait_ge(s_tab, 2)
            pool.wait_ge(s_hrows, 80)
            for b in range(NB):
                if b + XG + 2 < NB:
                    gather(b + XG + 2)
                scatter(b)


def kernel(x, x_txt, L0_tok_W, L0_tok_b, L0_txt_weight_l, L0_txt_weight_r, L0_attn_W_q, L0_attn_W_k, L0_attn_W_v,
           L0_attn_W_gate, L0_attn_b_gate, L0_attn_W_o, L0_ffn_Wg, L0_ffn_W1, L0_ffn_b1, L0_ffn_W2, L0_ffn_b2):
    import concourse.bacc as bacc
    from concourse.bass_utils import run_bass_kernel_spmd as run

    a = np.asarray
    c = np.ascontiguousarray
    runs = a(x).transpose(0, 2, 1, 3).reshape(2, HB * NP, PC, P)

    def rows(w, n):
        w = a(w)
        return w.reshape(n, P, w.shape[-1]).transpose(1, 0, 2)

    mats = [a(w).reshape(DC, P, HP, P).transpose(2, 1, 0, 3).reshape(HP, P, DC * P)
            for w in (L0_attn_W_gate, L0_attn_W_k, L0_attn_W_q, L0_attn_W_v)]
    arrays = {
        "x_idx": c(a(x_txt).reshape(G, P).T),
        "patches": c(runs.transpose(0, 3, 2, 1)),
        "w_tok": c(rows(a(L0_tok_W).T, PC)),
        "b_tok": c(a(L0_tok_b).reshape(DC, P).T),
        "w_l": c(a(L0_txt_weight_l)),
        "w_r": c(a(L0_txt_weight_r)),
        "w_attn": np.concatenate([*mats, a(L0_attn_b_gate).reshape(HP, P, 1)], axis=2),
        "w_o": c(rows(L0_attn_W_o, HP)),
        "w_gate": c(rows(L0_ffn_Wg, DC)),
        "w_1": c(a(L0_ffn_W1).reshape(E, DC, P, FH).transpose(2, 0, 1, 3).reshape(P, E, WF)),
        "w_2": c(a(L0_ffn_W2).reshape(E, FC, P, D).transpose(2, 0, 1, 3).reshape(P, E, WF)),
        "b_1": c(a(L0_ffn_b1).reshape(E, FC, P).transpose(2, 0, 1)),
        "b_2": a(L0_ffn_b2).reshape(1, E * D),
    }
    nc = bacc.Bacc("TRN2", target_bir_lowering=False, num_devices=1)
    ins = {n: nc.dram_tensor(n, v.shape, mybir.dt.from_np(v.dtype), kind="ExternalInput").ap()
           for n, v in arrays.items()}
    out = nc.dram_tensor("out", (TOK + P, D), F32, kind="ExternalOutput").ap()
    xrows = nc.dram_tensor("xrows", (TOK, D), F32, kind="Internal").ap()
    build(nc, **ins, out=out, xrows=xrows)
    got = run(nc, [arrays], core_ids=[0]).results[0]["out"]
    return got[:TOK].reshape(B, T, D)
```
